# Optimizing a Trainium2 kernel written in Bass

```python
import numpy as np
import jax
import jax.numpy as jnp

def _softmax(x, axis=-1):
    return jax.nn.softmax(x, axis=axis)

def _gelu(x):
    return jax.nn.gelu(x, approximate=True)

def _silu(x):
    return jax.nn.silu(x)

def _sigmoid(x):
    return jax.nn.sigmoid(x)

def _layernorm(x, axis=-1, eps=1e-05):
    m = jnp.mean(x, axis=axis, keepdims=True)
    v = jnp.var(x, axis=axis, keepdims=True)
    return (x - m) / jnp.sqrt(v + eps)

def _scatter_add(tgt, idx, src, axis=0):
    return tgt.at[idx].add(src)

def _segment_sum(src, seg, n):
    return jax.ops.segment_sum(src, seg, n)
kernel_name = 'mk_early_fusion_d1_tok_img512_r4_9b5503'

def setup_inputs(seed: int=0):
    np.random.seed(seed)
    _w = jnp.asarray

    def _rec_inputs():
        import jax
        import jax.numpy as jnp
        _rk = jax.random.key(seed)
        x = -0.000356955 + 1 * jax.random.normal(jax.random.fold_in(_rk, 1), (16, 3, 224, 224), jnp.float32)
        txt = -3.85354e-11 + 0.999983 * jax.random.normal(jax.random.fold_in(_rk, 2), (16, 128, 128), jnp.float32)
        return (x, txt)
    x, txt = _rec_inputs()

    def _L0_tok_setup():
        import jax, jax.numpy as jnp
        import numpy as np
        P = 16
        SHIFT = P // 2
        EPS = 1e-05

        def _shift2d(img, dy, dx):
            H, W = (img.shape[2], img.shape[3])
            pad = ((0, 0), (0, 0), (max(dy, 0), max(-dy, 0)), (max(dx, 0), max(-dx, 0)))
            z = jnp.pad(img, pad)
            return z[:, :, max(-dy, 0):max(-dy, 0) + H, max(-dx, 0):max(-dx, 0) + W]

        def _patchify(img):
            B, C, H, W = img.shape
            nH, nW = (H // P, W // P)
            t = img.reshape(B, C, nH, P, nW, P).transpose(0, 2, 4, 1, 3, 5)
            return t.reshape(B, nH * nW, C * P * P)
        key = jax.random.key(seed)
        ks = jax.random.split(key, 8)
        B, C, H, Wd = (128, 3, 224, 224)
        embed_dim = 128
        d_main = embed_dim // 2
        d_shift = embed_dim // 8
        fan_in = C * P * P
        std = 0.02
        x = jax.random.normal(ks[0], (B, C, H, Wd), dtype=jnp.float32)
        W_main = jax.random.normal(ks[1], (d_main, fan_in), dtype=jnp.float32) * std
        b_main = jnp.zeros((d_main,), dtype=jnp.float32)
        W_sx = jax.random.normal(ks[2], (d_shift, fan_in), dtype=jnp.float32) * std
        b_sx = jnp.zeros((d_shift,), dtype=jnp.float32)
        W_sy = jax.random.normal(ks[3], (d_shift, fan_in), dtype=jnp.float32) * std
        b_sy = jnp.zeros((d_shift,), dtype=jnp.float32)
        ln_g = jnp.ones((embed_dim,), dtype=jnp.float32)
        ln_b = jnp.zeros((embed_dim,), dtype=jnp.float32)
        return {'x': x, 'W_main': W_main, 'b_main': b_main, 'W_sx': W_sx, 'b_sx': b_sx, 'W_sy': W_sy, 'b_sy': b_sy, 'ln_g': ln_g, 'ln_b': ln_b}
    _L0_tok_all = _L0_tok_setup()
    _L0_tok_in = {k: v for k, v in _L0_tok_all.items() if k in ('W_main', 'b_main', 'W_sx', 'b_sx', 'W_sy', 'b_sy', 'ln_g', 'ln_b')}
    del _L0_tok_all

    def _L0_attn_setup():
        import jax, jax.numpy as jnp
        import numpy as np
        GAMMA = 0.9
        NUM_HEADS = 8
        SCALE_BASE = 512.0
        GN_EPS = 1e-05

        def xpos(x):
            B, S, D = x.shape
            half = D // 2
            scale_vec = (jnp.arange(0, D, 2, dtype=jnp.float32) + 0.4 * D) / (1.4 * D)
            power = jnp.arange(S, dtype=jnp.float32) / SCALE_BASE
            scale = scale_vec[None, :] ** power[:, None]
            inv_freq = 1.0 / 10000.0 ** (jnp.arange(half, dtype=jnp.float32) / half)
            sinusoid = jnp.arange(S, dtype=jnp.float32)[:, None] * inv_freq[None, :]
            sin_s = jnp.repeat(jnp.sin(sinusoid) * scale, 2, axis=-1)
            cos_s = jnp.repeat(jnp.cos(sinusoid) * scale, 2, axis=-1)
            x1, x2 = (x[..., ::2], x[..., 1::2])
            rot = jnp.stack([-x2, x1], axis=-1).reshape(x.shape)
            return x * cos_s[None] + rot * sin_s[None]

        def group_norm(x, weight, bias, num_groups):
            N, C = x.shape
            xg = x.reshape(N, num_groups, C // num_groups)
            mu = jnp.mean(xg, axis=-1, keepdims=True)
            var = jnp.var(xg, axis=-1, keepdims=True)
            xn = ((xg - mu) * jax.lax.rsqrt(var + GN_EPS)).reshape(N, C)
            return xn * weight[None, :] + bias[None, :]

        def decay_matrix(S):
            n = jnp.arange(S, dtype=jnp.float32)[:, None]
            m = jnp.arange(S, dtype=jnp.float32)[None, :]
            return jnp.where(n >= m, GAMMA ** (n - m), 0.0)
        key = jax.random.key(seed)
        ks = jax.random.split(key, 6)
        B, S, Din, Dm = (2, 512, 128, 128)
        s = 1.0 / np.sqrt(Din)
        return {'X': jax.random.normal(ks[0], (B, S, Din), dtype=jnp.float32), 'Wq': jax.random.uniform(ks[1], (Din, Dm), jnp.float32, -s, s), 'Wk': jax.random.uniform(ks[2], (Din, Dm), jnp.float32, -s, s), 'Wv': jax.random.uniform(ks[3], (Din, Dm), jnp.float32, -s, s), 'gn_weight': jnp.ones((Dm,), jnp.float32), 'gn_bias': jnp.zeros((Dm,), jnp.float32)}
    _L0_attn_all = _L0_attn_setup()
    _L0_attn_in = {k: v for k, v in _L0_attn_all.items() if k in ('Wq', 'Wk', 'Wv', 'gn_weight', 'gn_bias')}
    del _L0_attn_all

    def _L0_ffn_setup():
        import jax, jax.numpy as jnp
        import numpy as np
        E = 8
        K = 1
        D = 128
        I = 512
        B, T = (2, 512)
        key = jax.random.key(seed)
        ks = jax.random.split(key, 7)
        s = 0.02
        x = jax.random.normal(ks[0], (B, T, D), jnp.float32)
        gate_w = jax.random.normal(ks[1], (E, D), jnp.float32) * s
        w1 = jax.random.normal(ks[2], (E, I, D), jnp.float32) * s
        w2 = jax.random.normal(ks[3], (E, D, I), jnp.float32) * s
        w3 = jax.random.normal(ks[4], (E, I, D), jnp.float32) * s
        sw1 = jax.random.normal(ks[5], (I, D), jnp.float32) * s
        sw2 = jax.random.normal(ks[6], (D, I), jnp.float32) * s
        return {'x': x, 'gate_w': gate_w, 'w1': w1, 'w2': w2, 'w3': w3, 'sw1': sw1, 'sw2': sw2}
    _L0_ffn_all = _L0_ffn_setup()
    _L0_ffn_in = {k: v for k, v in _L0_ffn_all.items() if k in ('gate_w', 'w1', 'w2', 'w3', 'sw1', 'sw2')}
    del _L0_ffn_all
    return {'x': x, 'txt': txt, 'L0_tok_W_main': _L0_tok_in['W_main'], 'L0_tok_b_main': _L0_tok_in['b_main'], 'L0_tok_W_sx': _L0_tok_in['W_sx'], 'L0_tok_b_sx': _L0_tok_in['b_sx'], 'L0_tok_W_sy': _L0_tok_in['W_sy'], 'L0_tok_b_sy': _L0_tok_in['b_sy'], 'L0_tok_ln_g': _L0_tok_in['ln_g'], 'L0_tok_ln_b': _L0_tok_in['ln_b'], 'L0_attn_Wq': _L0_attn_in['Wq'], 'L0_attn_Wk': _L0_attn_in['Wk'], 'L0_attn_Wv': _L0_attn_in['Wv'], 'L0_attn_gn_weight': _L0_attn_in['gn_weight'], 'L0_attn_gn_bias': _L0_attn_in['gn_bias'], 'L0_ffn_gate_w': _L0_ffn_in['gate_w'], 'L0_ffn_w1': _L0_ffn_in['w1'], 'L0_ffn_w2': _L0_ffn_in['w2'], 'L0_ffn_w3': _L0_ffn_in['w3'], 'L0_ffn_sw1': _L0_ffn_in['sw1'], 'L0_ffn_sw2': _L0_ffn_in['sw2']}

def reference(x, txt, L0_tok_W_main, L0_tok_b_main, L0_tok_W_sx, L0_tok_b_sx, L0_tok_W_sy, L0_tok_b_sy, L0_tok_ln_g, L0_tok_ln_b, L0_attn_Wq, L0_attn_Wk, L0_attn_Wv, L0_attn_gn_weight, L0_attn_gn_bias, L0_ffn_gate_w, L0_ffn_w1, L0_ffn_w2, L0_ffn_w3, L0_ffn_sw1, L0_ffn_sw2):
    import jax
    import jax.numpy as jnp

    def _L0_tok_ref(x, W_main, b_main, W_sx, b_sx, W_sy, b_sy, ln_g, ln_b):
        import jax, jax.numpy as jnp
        import numpy as np
        P = 16
        SHIFT = P // 2
        EPS = 1e-05

        def _shift2d(img, dy, dx):
            H, W = (img.shape[2], img.shape[3])
            pad = ((0, 0), (0, 0), (max(dy, 0), max(-dy, 0)), (max(dx, 0), max(-dx, 0)))
            z = jnp.pad(img, pad)
            return z[:, :, max(-dy, 0):max(-dy, 0) + H, max(-dx, 0):max(-dx, 0) + W]

        def _patchify(img):
            B, C, H, W = img.shape
            nH, nW = (H // P, W // P)
            t = img.reshape(B, C, nH, P, nW, P).transpose(0, 2, 4, 1, 3, 5)
            return t.reshape(B, nH * nW, C * P * P)

        def proj(img, W, b):
            return jnp.einsum('bnf,of->bno', _patchify(img), W) + b
        main = proj(x, W_main, b_main)
        xl = proj(_shift2d(x, 0, -SHIFT), W_sx, b_sx)
        xr = proj(_shift2d(x, 0, SHIFT), W_sx, b_sx)
        yu = proj(_shift2d(x, -SHIFT, 0), W_sy, b_sy)
        yd = proj(_shift2d(x, SHIFT, 0), W_sy, b_sy)
        tok = jnp.concatenate([main, xl, xr, yu, yd], axis=-1)
        mu = jnp.mean(tok, axis=-1, keepdims=True)
        var = jnp.mean(jnp.square(tok - mu), axis=-1, keepdims=True)
        return (tok - mu) * jax.lax.rsqrt(var + EPS) * ln_g + ln_b

    def _L0_attn_ref(X, Wq, Wk, Wv, gn_weight, gn_bias):
        import jax, jax.numpy as jnp
        import numpy as np
        GAMMA = 0.9
        NUM_HEADS = 8
        SCALE_BASE = 512.0
        GN_EPS = 1e-05

        def xpos(x):
            B, S, D = x.shape
            half = D // 2
            scale_vec = (jnp.arange(0, D, 2, dtype=jnp.float32) + 0.4 * D) / (1.4 * D)
            power = jnp.arange(S, dtype=jnp.float32) / SCALE_BASE
            scale = scale_vec[None, :] ** power[:, None]
            inv_freq = 1.0 / 10000.0 ** (jnp.arange(half, dtype=jnp.float32) / half)
            sinusoid = jnp.arange(S, dtype=jnp.float32)[:, None] * inv_freq[None, :]
            sin_s = jnp.repeat(jnp.sin(sinusoid) * scale, 2, axis=-1)
            cos_s = jnp.repeat(jnp.cos(sinusoid) * scale, 2, axis=-1)
            x1, x2 = (x[..., ::2], x[..., 1::2])
            rot = jnp.stack([-x2, x1], axis=-1).reshape(x.shape)
            return x * cos_s[None] + rot * sin_s[None]

        def group_norm(x, weight, bias, num_groups):
            N, C = x.shape
            xg = x.reshape(N, num_groups, C // num_groups)
            mu = jnp.mean(xg, axis=-1, keepdims=True)
            var = jnp.var(xg, axis=-1, keepdims=True)
            xn = ((xg - mu) * jax.lax.rsqrt(var + GN_EPS)).reshape(N, C)
            return xn * weight[None, :] + bias[None, :]

        def decay_matrix(S):
            n = jnp.arange(S, dtype=jnp.float32)[:, None]
            m = jnp.arange(S, dtype=jnp.float32)[None, :]
            return jnp.where(n >= m, GAMMA ** (n - m), 0.0)
        B, S, Din = X.shape
        Dm = Wq.shape[1]
        H = NUM_HEADS
        hd = Dm // H
        q = xpos(X @ Wq)
        k = xpos(X @ Wk)
        k = group_norm(k.reshape(-1, Dm), gn_weight, gn_bias, H).reshape(B, S, Dm)
        v = X @ Wv
        q = q.reshape(B, S, H, hd).transpose(0, 2, 1, 3)
        k = k.reshape(B, S, H, hd).transpose(0, 2, 1, 3)
        v = v.reshape(B, S, H, hd).transpose(0, 2, 1, 3)
        q = q * jax.nn.sigmoid(q)
        scores = jnp.einsum('bhsd,bhtd->bhst', q, k)
        msr = scores * decay_matrix(S)[None, None]
        out = jnp.einsum('bhst,bhtd->bhsd', msr, v)
        out = out.transpose(0, 2, 1, 3).reshape(B, S, Dm)
        out = out + X
        return jax.nn.relu(out)

    def _L0_ffn_ref(x, gate_w, w1, w2, w3, sw1, sw2):
        import jax, jax.numpy as jnp
        import numpy as np
        E = 8
        K = 1
        D = 128
        I = 512
        B, T = (2, 512)
        xf = x.reshape(-1, D)
        logits = xf @ gate_w.T
        wts, idx = jax.lax.top_k(logits, K)
        wts = jax.nn.softmax(wts, axis=-1)
        comb = jnp.einsum('nke,nk->ne', jax.nn.one_hot(idx, E, dtype=xf.dtype), wts)
        h = jax.nn.silu(jnp.einsum('nd,eid->nei', xf, w1)) * jnp.einsum('nd,eid->nei', xf, w3)
        y = jnp.einsum('nei,edi->nd', h * comb[:, :, None], w2)
        y = y + jax.nn.gelu(xf @ sw1.T, approximate=False) @ sw2.T
        return y.reshape(x.shape)
    h = _L0_tok_ref(x, L0_tok_W_main, L0_tok_b_main, L0_tok_W_sx, L0_tok_b_sx, L0_tok_W_sy, L0_tok_b_sy, L0_tok_ln_g, L0_tok_ln_b)
    h = jnp.concatenate([h, txt], axis=1)
    h = h + _L0_attn_ref(_layernorm(h, axis=-1), L0_attn_Wq, L0_attn_Wk, L0_attn_Wv, L0_attn_gn_weight, L0_attn_gn_bias)
    h = h + _L0_ffn_ref(_layernorm(h, axis=-1), L0_ffn_gate_w, L0_ffn_w1, L0_ffn_w2, L0_ffn_w3, L0_ffn_sw1, L0_ffn_sw2)
    return h

_drawn_inputs = setup_inputs


def setup_inputs(seed=0):
    import zlib

    import numpy as np

    out = dict(_drawn_inputs(seed))
    spreads = {'L0_tok_b_main': (0.0, 0.1),
     'L0_tok_b_sx': (0.0, 0.1),
     'L0_tok_b_sy': (0.0, 0.1),
     'L0_tok_ln_g': (1.0, 0.2),
     'L0_tok_ln_b': (0.0, 0.1),
     'L0_attn_gn_weight': (1.0, 0.2),
     'L0_attn_gn_bias': (0.0, 0.1)}
    factors = {'L0_ffn_gate_w': 8.0,
     'L0_ffn_w1': 8.0,
     'L0_ffn_w2': 8.0,
     'L0_ffn_w3': 8.0,
     'L0_ffn_sw1': 8.0,
     'L0_ffn_sw2': 8.0}
    for name, (base, spread) in spreads.items():
        noise = np.random.default_rng([zlib.crc32(name.encode()), seed]).standard_normal(out[name].shape)
        drawn = base * np.exp(spread * noise) if base else spread * noise
        out[name] = jnp.asarray(drawn.astype(out[name].dtype))
    for name, factor in factors.items():
        out[name] = (out[name] * factor).astype(out[name].dtype)
    return out
```

```python
from contextlib import ExitStack

import numpy as np
import concourse.bass as bass
from concourse import mybir

F32 = mybir.dt.float32
I32 = mybir.dt.int32
U32 = mybir.dt.uint32
ALU = mybir.AluOpType
ACT = mybir.ActivationFunctionType
AX_X = mybir.AxisListType.X

P = 128
IMAGES = 16
GRID = 14
PATCHES = GRID * GRID
TEXT = 128
TOKENS = PATCHES + TEXT
HALF = PATCHES // 2
TILES = 3
WIDTH = (HALF, HALF, TEXT)
START = (0, HALF, PATCHES)
KC = 6
HEADS = 8
HD = P // HEADS
GAMMA = 0.9
EPS = 1e-5
EXPERTS = 8
INNER = 512
IC = INNER // P
ALL_TILES = IMAGES * TILES
ALL_TOKENS = IMAGES * TOKENS
SLOT_TILES = (ALL_TOKENS + EXPERTS * (P - 1)) // P
SLOTS = SLOT_TILES * P
ROW = 260
ROW_ID = 2 * P
PAD_ID = 1 << 20

CONST_LAYOUT = [
    ("identity", P), ("causal", P), ("block_diag", P), ("before", P), ("ones", P),
    ("select_same", P), ("select_neighbours", 4 * HD), ("cos", TILES * P), ("sin", TILES * P),
    ("gamma_neg", TILES), ("gamma_pos", TILES), ("head_of_four", 4),
    ("descending", EXPERTS), ("valid", TILES), ("tile_start", SLOT_TILES),
    ("minus_half", 2),
]
CONST_AT = {}
_at = 0
for _name, _n in CONST_LAYOUT:
    CONST_AT[_name] = (_at, _at + _n)
    _at += _n
CONST_COLS = _at
PAR_LAYOUT = [("patch_bias", 1), ("near_bias", 1), ("ln_g", P), ("ln_b", P), ("gn_w", P), ("gn_b", P), ("gate", EXPERTS)]
PAR_AT = {}
_at = 0
for _name, _n in PAR_LAYOUT:
    PAR_AT[_name] = (_at, _at + _n)
    _at += _n
PAR_COLS = _at


def build(nc, x, txt, patch_w, params, w_qkv, w1, w3, w2, sw1, sw2, consts, out):
    ctx = ExitStack()
    with ctx:
        def sb(name, shape, dt=F32):
            return ctx.enter_context(nc.sbuf_tensor(name, shape, dt))

        def ps(name, shape):
            return ctx.enter_context(nc.psum_tensor(name, shape, F32))

        def sem(name):
            return ctx.enter_context(nc.semaphore(name))

        sorted_rows = nc.dram_tensor("sorted_rows", [SLOTS, ROW], F32, kind="Internal").ap()
        out_rows = out.rearrange("b t d -> (b t) d")

        const_sb = sb("const_sb", [P, CONST_COLS])

        def const(name):
            a, b = CONST_AT[name]
            return const_sb[:, a:b]

        par_sb = sb("par_sb", [P, PAR_COLS])

        def par(name):
            a, b = PAR_AT[name]
            return par_sb[:, a:b]

        patch_w_sb = sb("patch_w_sb", [P, KC, P])
        qkv_w_sb = sb("qkv_w_sb", [P, 3 * P])
        w1_sb = sb("w1_sb", [P, EXPERTS * INNER])
        w3_sb = sb("w3_sb", [P, EXPERTS * INNER])
        w2_sb = sb("w2_sb", [P, EXPERTS * INNER])
        sw1_sb = sb("sw1_sb", [P, INNER])
        sw2_sb = sb("sw2_sb", [P, IC, P])
        rows = sb("rows", [P, ALL_TILES, ROW])
        normed_t_all = sb("normed_t_all", [P, ALL_TOKENS])
        pad_row = sb("pad_row", [P, ROW])

        x_sb = sb("x_sb", [P, 2, KC, PATCHES])
        grid_sb = sb("grid_sb", [P, 2, PATCHES])
        near_sb = sb("near_sb", [P, 2, GRID, GRID])
        tok_norm = sb("tok_norm", [P, 2, P])
        tok_scaled = sb("tok_scaled", [P, 2, P])
        token_buf = sb("token_buf", [P, 4 * TILES * P])
        token_view = token_buf[:, :].rearrange("p (k b t n) -> p k b t n", k=2, b=2, t=TILES)
        xin = token_view[:, 0, :, :, :]
        normed = token_view[:, 1, :, :, :]
        xin_t = sb("xin_t", [P, TILES, P])
        rot_a = sb("rot_a", [P, 2, 2, P])
        rot_b = sb("rot_b", [P, 2, 2, P])
        qk = sb("qk", [P, 2, 2, TILES, P])
        v_pad = sb("v_pad", [P, 2, TILES, HEADS, 2 * HD])
        gn_sum = sb("gn_sum", [P, TILES * HEADS])
        gn_mean = sb("gn_mean", [P, TILES * HEADS])
        gn_sq = sb("gn_sq", [P, TILES * P])
        gn_var = sb("gn_var", [P, TILES * HEADS])
        k_cent = sb("k_cent", [P, TILES, P])
        q_t = sb("q_t", [P, TILES, P])
        k_t = sb("k_t", [P, TILES, P])
        state = sb("state", [P, 2, P])
        work = sb("work", [P, 2 * HEADS * P + 4 * TILES * P])
        probs = work[:, 0:2 * HEADS * P].rearrange("p (b h n) -> p b h n", b=2, h=HEADS)
        q_four = work[:, 2 * HEADS * P:].rearrange("p (t e n) -> p t e n", t=TILES, e=4)
        mix_t = sb("mix_t", [P, 2, P])
        mixed = sb("mixed", [P, TILES, P])
        normed_t = sb("normed_t", [P, TILES, P])
        stats = sb("stats", [P, 3, TILES, 6])
        meanvar = sb("meanvar", [P, 3, TILES, 2])
        tok_var = sb("tok_var", [P, 2])
        tok_rstd = sb("tok_rstd", [P, 2])
        NORMS = 2 * TILES + TILES * HEADS
        var_sb = sb("var_sb", [P, NORMS])
        guess = sb("guess", [P, NORMS])
        square = sb("square", [P, NORMS])
        rstd = sb("rstd", [P, NORMS])
        logits = sb("logits", [P, ALL_TILES, EXPERTS])

        gelu_sb = work[:, 0:2 * IC * TOKENS].rearrange("p (b c n) -> p b c n", b=2, c=IC)
        row_c = token_buf[:, 0:4 * ROW].rearrange("p (b c) -> p b c", b=4)
        qk_flat = qk[:, :, :, :, :].rearrange("p b a t n -> p (b a t n)")
        fin_c = qk_flat[:, 2 * INNER:2 * INNER + 4 * P].rearrange("p (b n) -> p b n", b=4)
        row_t = sb("row_t", [P, 2, P])
        x_flat = x_sb[:, :, :, :].rearrange("p b k n -> p (b k n)")
        silu_c = x_flat[:, 0:2 * INNER].rearrange("p (b n) -> p b n", b=2)
        gated = x_flat[:, 2 * INNER:4 * INNER].rearrange("p (b n) -> p b n", b=2)
        gated_t = qk_flat[:, 0:2 * INNER].rearrange("p (b n) -> p b n", b=2)
        v_flat = v_pad[:, :, :, :, :].rearrange("p b t h c -> p (b t h c)")
        TABLE = ALL_TILES * EXPERTS
        rt_m = sb("rt_m", [P, ALL_TILES])
        rt_eq = k_cent[:, :, :].rearrange("p t c -> p (t c)") \
            .rearrange("p (t e) -> p t e", e=EXPERTS)
        rt_cand = v_flat[:, 0:TABLE].rearrange("p (t e) -> p t e", e=EXPERTS)
        rt_best = sb("rt_best", [P, ALL_TILES])
        rt_hit = v_flat[:, TABLE:2 * TABLE].rearrange("p (t e) -> p t e", e=EXPERTS)
        onehot = sb("onehot", [P, ALL_TILES, EXPERTS])
        rt_tot = v_flat[:, 2 * TABLE:3 * TABLE].rearrange("p (e t) -> p e t", e=EXPERTS)
        rt_zero = v_flat[:, 3 * TABLE:4 * TABLE]
        rt_cum = gn_sq[:, :] \
            .rearrange("p (e t) -> p e t", e=EXPERTS)
        rt_exc = token_buf[:, 0:TABLE].rearrange("p (e t) -> p e t", e=EXPERTS)
        rt_n = sb("rt_n", [P, EXPERTS])
        rt_int = sb("rt_int", [P, EXPERTS], I32)
        rt_mod = sb("rt_mod", [P, EXPERTS], I32)
        rt_pad = sb("rt_pad", [P, EXPERTS])
        rt_end = sb("rt_end", [P, EXPERTS])
        rt_off = sb("rt_off", [P, EXPERTS])
        rt_off2 = sb("rt_off2", [P, EXPERTS])
        rt_base = token_buf[:, TABLE:2 * TABLE].rearrange("p (e t) -> p e t", e=EXPERTS)
        rt_pos = rot_a[:, :, :, :].rearrange("p a b c -> p (a b c)")[:, 0:ALL_TILES * EXPERTS] \
            .rearrange("p (t e) -> p t e", e=EXPERTS)
        rt_posf = sb("rt_posf", [P, ALL_TILES])
        slot_of = sb("slot_of", [P, ALL_TILES], I32)
        rt_ge = rot_b[:, :, :, :].rearrange("p a b c -> p (a b c)")[:, 0:SLOT_TILES * EXPERTS] \
            .rearrange("p (t e) -> p t e", e=EXPERTS)
        rt_te = gn_sq[:, 0:SLOT_TILES]
        expert_of_tile = sb("expert_of_tile", [P, SLOT_TILES], I32)

        bank = [ps(f"bank{i}", [P, 512]) for i in range(4)]
        quad = ps("quad", [P, 4, 512])
        patch_ps = bank[0][:, 0:PATCHES]
        tok_ps = bank[0][:, 256:512].rearrange("p (t c) -> p t c", t=2)
        xt_ps = bank[1][:, 0:TILES * P]
        qkv_ps = bank[2][:, 0:3 * P]
        back_ps = bank[1][:, TILES * P:4 * P]
        mix_ps = bank[3][:, 0:P]
        gate_ps = bank[3][:, P:P + TILES * EXPERTS]
        kt_ps = quad[:, 0, 0:TILES * P]
        state_ps = quad[:, 1, 0:2 * P]
        qt_ps = quad[:, 2, 0:TILES * P]

        def score_ps(t):
            w = WIDTH[t]
            a = 2 * (t % 2)
            return quad[0:w, a:a + 2, 0:4 * w].rearrange("p g (e n) -> p g e n", e=4)

        row_t_ps = bank[0][:, 0:P]
        silu_ps = [bank[1][:, :], bank[2][:, :]]
        gate_ps_c = [bank[3][:, :], quad[:, 0, :]]
        gated_t_ps = quad[:, 1, :]
        down_ps = [quad[:, 2, 0:P], quad[:, 3, 0:P]]

        names = """const_in par_in w_in qkvw_in txt_in expert_in shared_in
            pad_made pad_written rows_tail grid_init xin_init
            patch_done grid_done tok_done tok_stat tok_meanvar tok_rstd_s tok_normed tok_scaled_s h_done
            ln1_stat ln1_meanvar xin_done norm_vars newton v_init xt_done xt_copied
            qkv_done rot_done v_done qk_done gn_sum_s gn_mean_s k_cent_s gn_sq_s gn_var_s tok_vareps
            k_norm_s k_scaled_s k_done
            qkt_done q_four_s q_t_s k_t_s state_done state_masked scores_done probs_done mix_done mix_copied back_done mixed_s h2_done
            ln2_stat ln2_meanvar normed_s nt_done nt_copied gate_done logits_done
            route_step onehot_s rank_done pos_done settled rows_sent expert_of_tile_s
            hid_done gelu_done shared_done base_done
            row_t_done row_t_copied up_done silu_done gated_s gt_done gt_copied down_done fin_done
            """.split()
        s = {n: sem(n) for n in names}
        x_in = [sem(f"x_in{b}") for b in range(2)]
        norm_moved = [sem(f"norm_moved{b}") for b in range(2)]
        row_in = [sem(f"row_in{b}") for b in range(4)]
        out_sent = [sem(f"out_sent{b}") for b in range(4)]

        def settle(eng):
            eng.sem_inc(s["settled"], 1)

        def number(im):
            return 2 * im[0] + im[1]

        def half_number(im):
            return im[0] + im[1] // 2

        def parity(im):
            return im[1] % 2

        def back(im, d):
            return (im[0], im[1] - d)

        def value(im, per, k):
            return 2 * per * im[0] + (per * im[1] + k)

        def first(im, d):
            return type(im[0]) is int and 2 * im[0] + im[1] < d

        STAGES = (("A", 0), ("Q", 1), ("S", 2), ("L", 3), ("G", 4))
        LAST = STAGES[-1][1]
        PEELED = 6

        def run_images(eng, step):
            def one(im, n=None):
                stages = {"step": im}
                for name, lag in STAGES:
                    if n is None or 0 <= n - lag < IMAGES:
                        stages[name] = back(im, lag)
                step(stages)
            for n in range(PEELED):
                one((0, n), n)
            with eng.Fori(PEELED // 2, IMAGES // 2) as m:
                one((m, 0))
                one((m, 1))
            for n in range(IMAGES, IMAGES + LAST):
                one((0, n), n)

        NEWTON = 11

        block = ctx.enter_context(nc.Block())

        @block.sync
        def _(sp):
            sp.dma_start(const_sb[:, :], consts).then_inc(s["const_in"], 16)
            sp.dma_start(patch_w_sb[:, :, :], patch_w).then_inc(s["w_in"], 16)
            for b in range(2):
                sp.dma_start(x_sb[:, b, :, :], x[b]).then_inc(x_in[b], 16)
            sp.dma_start(par_sb[:, :], params).then_inc(s["par_in"], 16)
            sp.dma_start(rows[:, TILES - 1:ALL_TILES:TILES, P:2 * P],
                         txt.rearrange("b t d -> t b d")).then_inc(s["txt_in"], 16)
            sp.dma_start(qkv_w_sb[:, :], w_qkv).then_inc(s["qkvw_in"], 16)
            def load_x(im):
                sp.wait_ge(s["patch_done"], value(im, 1, 1))
                sp.dma_start(x_sb[:, parity(im), :, :],
                             x[bass.ds(number(im) + 2, 1)].rearrange("o p k n -> (o p) k n")
                             ).then_inc(x_in[parity(im)], 16)

            def move(im):
                sp.wait_ge(s["normed_s"], value(im, 1, 1))
                sp.dma_start(rows[:, bass.ds(number(im) * TILES, TILES), 0:P],
                             normed[:, parity(im), :, :]).then_inc(norm_moved[parity(im)], 16)
                sp.wait_ge(s["nt_copied"], value(im, 1, 1))
                sp.dma_start(normed_t_all[:, bass.ds(number(im) * TOKENS, 2 * HALF)]
                             .rearrange("p (t n) -> p t n", t=2),
                             normed_t[:, 0:2, 0:HALF]).then_inc(norm_moved[parity(im)], 16)
                sp.dma_start(normed_t_all[:, bass.ds(number(im) * TOKENS + 2 * HALF, TEXT)],
                             normed_t[:, 2, :]).then_inc(norm_moved[parity(im)], 16)

            load_x((0, 0))
            sp.wait_ge(s["pad_made"], 3)
            sp.dma_start(sorted_rows.rearrange("(j p) c -> p j c", p=P),
                         pad_row[:, :].unsqueeze(1).broadcast_to([P, SLOT_TILES, ROW])
                         ).then_inc(s["pad_written"], 16)
            load_x((0, 1))
            sp.dma_start(w1_sb[:, :], w1).then_inc(s["expert_in"], 16)
            load_x((0, 2))
            sp.dma_start(w3_sb[:, :], w3).then_inc(s["expert_in"], 16)
            load_x((0, 3))
            sp.dma_start(w2_sb[:, :], w2).then_inc(s["expert_in"], 16)
            sp.dma_start(sw1_sb[:, :], sw1).then_inc(s["shared_in"], 16)
            sp.dma_start(sw2_sb[:, :, :], sw2).then_inc(s["shared_in"], 16)
            with sp.Fori(2, IMAGES // 2 - 1) as m:
                for off in range(2):
                    load_x((m, off))
                    move((m, off - 4))
            for i in range(IMAGES - 6, IMAGES):
                move((0, i))

            sp.wait_ge(s["pad_written"], 16)
            sp.wait_ge(s["rows_sent"], 16 * ALL_TILES)

            def load_rows(m, off, free):
                if free:
                    sp.wait_ge(out_sent[off], 16 * m)
                sp.dma_start(row_c[:, off, :],
                             sorted_rows[bass.ds((4 * m + off) * P, P), :]).then_inc(row_in[off], 16)

            for off in range(4):
                load_rows(0, off, False)
            with sp.Fori(1, SLOT_TILES // 4) as m:
                for off in range(4):
                    load_rows(m, off, True)
            for off in range(4):
                sp.wait_ge(out_sent[off], 16 * (SLOT_TILES // 4))

        @block.gpsimd
        def _(pool):
            nc.gpsimd.memset(pad_row[:, :], 0.0).then_inc(s["pad_made"], 1)
            pool.wait_ge(s["pad_made"], 1)
            nc.gpsimd.iota(pad_row[:, ROW_ID:ROW_ID + 1].bitcast(I32), pattern=[[0, 1]],
                           base=PAD_ID, channel_multiplier=1).then_inc(s["pad_made"], 1)
            nc.gpsimd.memset(rows[:, :, ROW_ID + 1:ROW], 0.0).then_inc(s["rows_tail"], 1)
            nc.gpsimd.iota(rows[:, :, ROW_ID:ROW_ID + 1].bitcast(I32)
                           .rearrange("p (b t) o -> p b t o", t=TILES),
                           pattern=[[TOKENS, IMAGES], [HALF, TILES], [0, 1]], base=0,
                           channel_multiplier=1).then_inc(s["rows_tail"], 1)
            nc.gpsimd.memset(rows[:, :, P:2 * P].rearrange("p (b t) c -> p b t c", t=TILES)
                             [:, :, 0:2, :], 0.0).then_inc(s["pad_made"], 1)
            nc.gpsimd.memset(mixed[:, :, :], 0.0).then_inc(s["xin_init"], 1)
            nc.gpsimd.memset(v_pad[:, :, :, :, :], 0.0).then_inc(s["v_init"], 1)

            def bc_tiles(ap, n):
                return ap.unsqueeze(1).broadcast_to([ap.shape[0], n, P])

            def step(st):
                if "A" in st:
                    ia = st["A"]

                def rotated(tiles):
                    im = st["Q"]
                    b = parity(im)
                    for t in tiles:
                        pool.wait_ge(s["rot_done"], value(im, 2 * TILES, 2 * t + 2))
                        if not first(im, 2) and t == 0:
                            pool.wait_ge(s["state_done"], value(im, 1, -1))
                        nc.gpsimd.tensor_tensor(qk[:, b, :, t, :], rot_a[:, t % 2, :, :], rot_b[:, t % 2, :, :],
                                                ALU.add).then_inc(s["qk_done"], 1)
                if "Q" in st:
                    rotated((0, 1))
                if "A" in st:
                    im = ia
                    pool.wait_ge(s["tok_vareps"], value(im, 1, 1))
                    nc.gpsimd.tensor_tensor(tok_rstd[0:HALF, :], tok_var[0:HALF, :],
                                            const("minus_half")[0:HALF, :], ALU.pow).then_inc(s["tok_rstd_s"], 1)
                    pool.wait_ge(s["tok_normed"], value(im, 1, 1))
                    if first(im, 1):
                        pool.wait_ge(s["par_in"], 16)
                    nc.gpsimd.tensor_tensor(tok_scaled[0:HALF, :, :], tok_norm[0:HALF, :, :],
                                            bc_tiles(par("ln_g")[0:HALF, :], 2),
                                            ALU.mult).then_inc(s["tok_scaled_s"], 1)
                    pool.wait_ge(s["tok_scaled_s"], value(im, 1, 1))
                    if first(im, 1):
                        pool.wait_ge(s["pad_made"], 3)
                    nc.gpsimd.tensor_tensor(rows[0:HALF, bass.ds(number(im) * TILES, 2), P:2 * P],
                                            tok_scaled[0:HALF, :, :],
                                            bc_tiles(par("ln_b")[0:HALF, :], 2),
                                            ALU.add).then_inc(s["h_done"], 1)
                if "Q" in st:
                    rotated((2,))
                    im = st["Q"]
                    b = parity(im)
                    kk = qk[:, b, 1, :, :].rearrange("p t (g d) -> p (t g) d", d=HD)
                    cent = k_cent[:, :, :].rearrange("p t (g d) -> p (t g) d", d=HD)

                    def over_group(ap):
                        return ap.unsqueeze(2).broadcast_to([P, TILES * HEADS, HD])
                    pool.wait_ge(s["gn_mean_s"], value(im, 1, 1))
                    nc.gpsimd.tensor_tensor(cent, kk, over_group(gn_mean[:, :]),
                                            ALU.subtract).then_inc(s["k_cent_s"], 1)
                    pool.wait_ge(s["newton"], value(st["step"], NEWTON, NEWTON))
                    pool.wait_ge(s["k_cent_s"], value(im, 1, 1))
                    nc.gpsimd.tensor_tensor(cent, cent, over_group(rstd[:, 2 * TILES:NORMS]),
                                            ALU.mult).then_inc(s["k_norm_s"], 1)
                    pool.wait_ge(s["k_norm_s"], value(im, 1, 1))
                    nc.gpsimd.tensor_tensor(k_cent[:, :, :], k_cent[:, :, :], bc_tiles(par("gn_w"), TILES),
                                            ALU.mult).then_inc(s["k_scaled_s"], 1)
                    pool.wait_ge(s["k_scaled_s"], value(im, 1, 1))
                    nc.gpsimd.tensor_tensor(qk[:, b, 1, :, :], k_cent[:, :, :], bc_tiles(par("gn_b"), TILES),
                                            ALU.add).then_inc(s["k_done"], 1)

            pool.wait_ge(s["const_in"], 16)
            run_images(pool, step)

            pool.wait_ge(s["pos_done"], 1)
            pool.wait_ge(s["pad_written"], 16)
            pool.wait_ge(s["rows_tail"], 2)
            for b in range(2):
                pool.wait_ge(norm_moved[b], 48 * (IMAGES // 2))
            for i in range(IMAGES):
                for t in range(TILES):
                    j = TILES * i + t
                    pool.wait_ge(s["base_done"], j + 1)
                    nc.gpsimd.indirect_dma_start(
                        out=sorted_rows,
                        out_offset=bass.IndirectOffsetOnAxis(
                            ap=slot_of[0:WIDTH[t], j:j + 1].bitcast(U32), axis=0),
                        in_=rows[0:WIDTH[t], j, :], in_offset=None).then_inc(s["rows_sent"], 16)

            with pool.Fori(0, SLOT_TILES // 4) as m:
                for off in range(4):
                    pool.wait_ge(s["fin_done"], 4 * m + (off + 1))
                    settle(pool)
                    nc.gpsimd.indirect_dma_start(
                        out=out_rows,
                        out_offset=bass.IndirectOffsetOnAxis(
                            ap=row_c[:, off, ROW_ID:ROW_ID + 1].bitcast(U32), axis=0),
                        in_=fin_c[:, off, :],
                        in_offset=None,
                        bounds_check=ALL_TOKENS - 1, oob_is_err=False).then_inc(out_sent[off], 16)

        @block.scalar
        def _(act):
            def step(st):
                if "A" in st:
                    im = st["A"]
                    b = parity(im)
                    act.wait_ge(s["patch_done"], value(im, 1, 1))
                    if first(im, 1):
                        act.wait_ge(s["grid_init"], 2)
                    if not first(im, 2):
                        act.wait_ge(s["tok_done"], value(im, 1, -1))
                    bias = par("patch_bias")
                    nc.scalar.activation(grid_sb[:, b, :], patch_ps, ACT.Identity, bias=bias)
                    square_ps = patch_ps.rearrange("p (i j) -> p i j", i=GRID)
                    for dst, rows_to, rows_from, cols_to, cols_from, src in (
                            (64, (0, GRID), (0, GRID), (1, GRID), (0, GRID - 1), 64),
                            (96, (0, GRID), (0, GRID), (0, GRID - 1), (1, GRID), 96),
                            (0, (1, GRID), (0, GRID - 1), (0, GRID), (0, GRID), 64),
                            (32, (0, GRID - 1), (1, GRID), (0, GRID), (0, GRID), 96)):
                        ins = nc.scalar.activation(
                            near_sb[dst:dst + 32, b, rows_to[0]:rows_to[1], cols_to[0]:cols_to[1]],
                            square_ps[src:src + 32, rows_from[0]:rows_from[1], cols_from[0]:cols_from[1]],
                            ACT.Identity, bias=bias[src:src + 32])
                    ins.then_inc(s["grid_done"], 1)
                if "Q" in st:
                    im = st["Q"]
                    b = parity(im)
                    act.wait_ge(s["xt_done"], value(im, 1, 1))
                    if not first(im, 1):
                        act.wait_ge(s["qkv_done"], value(im, TILES, 0))
                    nc.scalar.activation(xin_t[:, :, :].rearrange("p t c -> p (t c)"), xt_ps,
                                         ACT.Copy).then_inc(s["xt_copied"], 1)

                    def v_copy(t):
                        act.wait_ge(s["rot_done"], value(im, 2 * TILES, 2 * t + 2))
                        if not first(im, 2) and t == 0:
                            act.wait_ge(s["mix_done"], value(im, TILES, -TILES))
                        mine = v_pad[:, b, t, :, :].rearrange("p (r e) c -> p r (e c)", e=2) \
                            .rearrange("p r (f d) -> p r f d", d=HD)[:, :, 0::3, :]
                        nc.scalar.activation(mine, qkv_ps[:, 2 * P:3 * P].rearrange("p (r e d) -> p r e d", e=2, d=HD),
                                             ACT.Identity,
                                             scale=const("gamma_neg")[:, t:t + 1]).then_inc(s["v_done"], 1)
                    v_copy(0)
                if "S" in st:
                    im2 = st["S"]
                    act.wait_ge(s["qkt_done"], value(im2, 2, 2))
                    if not first(im2, 1):
                        act.wait_ge(s["mix_done"], value(im2, TILES, 0))
                    q3 = qt_ps.rearrange("p (t n) -> p t n", t=TILES)
                    nc.scalar.activation(k_t[:, :, :].rearrange("p t c -> p (t c)"), kt_ps,
                                         ACT.Copy).then_inc(s["k_t_s"], 1)
                    for e in range(4):
                        nc.scalar.activation(q_four[:, :, e, :], q3, ACT.Silu,
                                             scale=const("head_of_four")[:, e:e + 1]).then_inc(s["q_four_s"], 1)
                    nc.scalar.activation(q_t[:, :, :], q3, ACT.Silu).then_inc(s["q_t_s"], 1)
                if "G" in st:
                    im3 = st["G"]
                    act.wait_ge(s["nt_done"], value(im3, 1, 1))
                    if not first(im3, 1):
                        act.wait_ge(s["gate_done"], value(im3, 1, 0))
                        before = back(im3, 1)
                        act.wait_ge(norm_moved[parity(before)], 48 * half_number(before) + 48)
                    nc.scalar.activation(normed_t[:, :, :].rearrange("p t c -> p (t c)"), xt_ps,
                                         ACT.Copy).then_inc(s["nt_copied"], 1)
                if "Q" in st:
                    v_copy(1)
                    v_copy(2)
                    act.wait_ge(s["k_cent_s"], value(im, 1, 1))
                    if not first(im, 1):
                        act.wait_ge(s["gn_var_s"], value(im, 1, 0))
                    nc.scalar.activation(gn_sq[:, :], k_cent[:, :, :].rearrange("p t c -> p (t c)"),
                                         ACT.Square).then_inc(s["gn_sq_s"], 1)
                if "S" in st:
                    for t in range(TILES):
                        w = WIDTH[t]
                        act.wait_ge(s["mix_done"], value(im2, TILES, t + 1))
                        if t > 1 or not first(im2, 1):
                            act.wait_ge(s["back_done"], value(im2, TILES, t - 1))
                        nc.scalar.activation(mix_t[:, t % 2, 0:w], mix_ps[:, 0:w],
                                             ACT.Copy).then_inc(s["mix_copied"], 1)

            act.wait_ge(s["const_in"], 16)
            act.wait_ge(s["par_in"], 16)
            act.wait_ge(s["v_init"], 1)
            run_images(act, step)

            def gelu(m, off, again):
                i = 2 * m + off
                for c in range(IC):
                    act.wait_ge(s["hid_done"], IC * i + (c + 1))
                    if again and c == 0:
                        act.wait_ge(s["shared_done"], i - 1)
                    nc.scalar.activation(gelu_sb[:, off, c, :], quad[:, c, 0:TOKENS],
                                         ACT.Gelu).then_inc(s["gelu_done"], 1)
            gelu(0, 0, False)
            gelu(0, 1, False)
            with act.Fori(1, IMAGES // 2) as m:
                gelu(m, 0, True)
                gelu(m, 1, True)

            def row_t_copy(j, b, again):
                act.wait_ge(s["row_t_done"], j + 1)
                if again:
                    act.wait_ge(s["up_done"], 2 * j - 2)
                nc.scalar.activation(row_t[:, b, :], row_t_ps,
                                     ACT.Copy).then_inc(s["row_t_copied"], 1)

            def silu(j, b, again):
                act.wait_ge(s["up_done"], 2 * j + 1)
                if again:
                    act.wait_ge(s["gated_s"], j - 1)
                nc.scalar.activation(silu_c[:, b, :], silu_ps[b], ACT.Silu).then_inc(s["silu_done"], 1)

            def gated_t_copy(j, b, again):
                act.wait_ge(s["gt_done"], j + 1)
                if again:
                    act.wait_ge(s["down_done"], j - 1)
                nc.scalar.activation(gated_t[:, b, :], gated_t_ps, ACT.Copy).then_inc(s["gt_copied"], 1)

            row_t_copy(0, 0, False)
            row_t_copy(1, 1, False)
            silu(0, 0, False)

            def tile_step(j, b, again, rows_ahead, next_silu):
                if rows_ahead:
                    row_t_copy(j + 2, b, True)
                gated_t_copy(j, b, again)
                if next_silu:
                    silu(j + 1, 1 - b, again)
            tile_step(0, 0, False, True, True)
            tile_step(1, 1, False, True, False)
            act.wait_ge(s["gated_s"], 1)
            silu(2, 0, False)
            with act.Fori(1, SLOT_TILES // 2 - 1) as m:
                for b in range(2):
                    tile_step(2 * m + b, b, True, True, True)
            tile_step(SLOT_TILES - 2, 0, True, False, True)
            tile_step(SLOT_TILES - 1, 1, True, False, False)

        @block.tensor
        def _(pe):
            ident = const("identity")

            def step(st):
                ia, iq, is_, ig = (st.get(n) for n in "AQSG")
                if ia:
                    b = parity(ia)
                    pe.wait_ge(x_in[b], 16 * half_number(ia) + 16)
                    if not first(ia, 1):
                        pe.wait_ge(s["tok_normed"], value(ia, 1, 0))
                    for k in range(KC):
                        mm = nc.tensor.matmul(patch_ps, patch_w_sb[:, k, :], x_sb[:, b, k, :],
                                              start=(k == 0), stop=(k == KC - 1))
                    mm.then_inc(s["patch_done"], 1)
                if iq:
                    pe.wait_ge(s["xin_done"], value(iq, 1, 1))
                    if not first(iq, 2):
                        pe.wait_ge(s["mixed_s"], value(iq, TILES, -TILES))
                    for t in range(TILES):
                        mm = nc.tensor.transpose(xt_ps[:, t * P:(t + 1) * P], xin[:, parity(iq), t, :], ident)
                    mm.then_inc(s["xt_done"], 1)

                def qkv(t):
                    if t > 0 or not first(iq, 1):
                        pe.wait_ge(s["rot_done"], value(iq, 2 * TILES, 2 * t))
                        pe.wait_ge(s["v_done"], value(iq, TILES, t))
                    nc.tensor.matmul(qkv_ps, xin_t[:, t, :], qkv_w_sb[:, :],
                                     start=True, stop=True).then_inc(s["qkv_done"], 1)
                if is_:
                    bs = parity(is_)

                    def v_of(t, w):
                        return v_pad[0:w, bs, t, :, :].rearrange("p (r e) c -> p r (e c)", e=2) \
                            .rearrange("p r (f d) -> p r f d", d=HD)[:, :, 0::3, :]
                    pe.wait_ge(s["k_done"], value(is_, 1, 1))
                    if not first(is_, 1):
                        pe.wait_ge(s["q_t_s"], value(is_, 1, 0))
                        pe.wait_ge(s["probs_done"], value(is_, TILES, 0))
                    for part, dst in ((1, kt_ps), (0, qt_ps)):
                        for t in range(TILES):
                            mm = nc.tensor.transpose(dst[:, t * P:(t + 1) * P], qk[:, bs, part, t, :], ident)
                        mm.then_inc(s["qkt_done"], 1)
                    pe.wait_ge(s["v_done"], value(is_, TILES, TILES))
                    for n in range(2):
                        for t in range(n + 1):
                            mm = nc.tensor.matmul(state_ps[:, n * P:(n + 1) * P],
                                                  qk[0:HALF, bs, 1, t, :], v_of(t, HALF),
                                                  start=(t == 0), stop=(t == n))
                    mm.then_inc(s["state_done"], 1)
                if iq:
                    pe.wait_ge(s["xt_copied"], value(iq, 1, 1))
                    if first(iq, 1):
                        pe.wait_ge(s["qkvw_in"], 16)
                    qkv(0)
                if ig:
                    pe.wait_ge(s["normed_s"], value(ig, 1, 1))
                    if not iq:
                        pe.wait_ge(s["xt_copied"], IMAGES)
                        pe.wait_ge(s["mixed_s"], TILES * IMAGES if not is_ else value(is_, TILES, 0))
                        if not first(ig, 1):
                            pe.wait_ge(s["nt_copied"], value(ig, 1, 0))
                    for t in range(TILES):
                        mm = nc.tensor.transpose(xt_ps[:, t * P:(t + 1) * P], normed[:, parity(ig), t, :], ident)
                    mm.then_inc(s["nt_done"], 1)
                if ia:
                    pe.wait_ge(s["grid_done"], value(ia, 1, 1))
                    for t in range(2):
                        at = START[t]
                        nc.tensor.matmul(tok_ps[0:HALF, t, :], grid_sb[:, b, at:at + HALF],
                                         const("select_same"), start=True, stop=False)
                        mm = nc.tensor.matmul(tok_ps[0:HALF, t, 4 * HD:8 * HD],
                                              near_sb[:, b, :, :].rearrange("p i j -> p (i j)")[:, at:at + HALF],
                                              const("select_neighbours"), start=False, stop=True)
                    mm.then_inc(s["tok_done"], 1)
                if iq:
                    qkv(1)

                def scores(t):
                    w = WIDTH[t]
                    for g in range(2):
                        rows_of = slice(64 * g, 64 * g + 64)
                        mm = nc.tensor.matmul(score_ps(t)[:, g, :, :], k_t[rows_of, t, 0:w],
                                              q_four[rows_of, t, :, 0:w], start=True, stop=True)
                    mm.then_inc(s["scores_done"], 1)

                def mix(t):
                    w = WIDTH[t]
                    if t > 0 or not first(is_, 1):
                        pe.wait_ge(s["mix_copied"], value(is_, TILES, t))
                    if t > 0:
                        nc.tensor.matmul(mix_ps[:, 0:w], state[:, t - 1, :], q_t[:, t, 0:w],
                                         start=True, stop=False)
                    pe.wait_ge(s["probs_done"], value(is_, TILES, t + 1))
                    for e in range(2):
                        for r in range(4):
                            mm = nc.tensor.matmul(mix_ps[32 * r:32 * r + 32, 0:w],
                                                  v_pad[0:w, bs, t, 2 * r + e, :], probs[0:w, t % 2, 2 * r + e, 0:w],
                                                  start=(t == 0 and e == 0), stop=(e == 1))
                    mm.then_inc(s["mix_done"], 1)

                def turn_back(t):
                    w = WIDTH[t]
                    pe.wait_ge(s["mix_copied"], value(is_, TILES, t + 1))
                    if t == 0:
                        if ig:
                            pe.wait_ge(s["nt_copied"], value(ig, 1, 1))
                        elif iq:
                            pe.wait_ge(s["xt_copied"], value(iq, 1, 1))
                    if t > 0 or not first(is_, 1):
                        pe.wait_ge(s["mixed_s"], value(is_, TILES, t))
                    nc.tensor.transpose(back_ps[0:w, :], mix_t[:, t % 2, 0:w], ident).then_inc(s["back_done"], 1)

                if is_:
                    pe.wait_ge(s["q_t_s"], value(is_, 1, 1))
                    pe.wait_ge(s["state_masked"], value(is_, 1, 1))
                    scores(0)
                    scores(1)
                if iq:
                    qkv(2)
                if ig:
                    pe.wait_ge(s["nt_copied"], value(ig, 1, 1))
                    if not first(ig, 1):
                        pe.wait_ge(s["logits_done"], value(ig, 1, 0))
                    if not is_:
                        pe.wait_ge(s["mix_copied"], TILES * IMAGES)
                    elif not first(is_, 1):
                        pe.wait_ge(s["mix_copied"], value(is_, TILES, 0))
                    for t in range(TILES):
                        mm = nc.tensor.matmul(gate_ps[:, t * EXPERTS:(t + 1) * EXPERTS],
                                              normed_t[:, t, :], par("gate"), start=True, stop=True)
                    mm.then_inc(s["gate_done"], 1)
                if is_:
                    if ig:
                        pe.wait_ge(s["logits_done"], value(ig, 1, 1))
                    mix(0)
                    scores(2)
                    mix(1)
                    turn_back(0)
                    mix(2)
                    turn_back(1)
                    turn_back(2)

            pe.wait_ge(s["const_in"], 16)
            pe.wait_ge(s["w_in"], 16)
            pe.wait_ge(s["par_in"], 16)
            run_images(pe, step)

            pe.wait_ge(s["shared_in"], 32)
            for b in range(2):
                pe.wait_ge(norm_moved[b], 48 * (IMAGES // 2))
            pe.wait_ge(s["probs_done"], TILES * IMAGES)
            pe.wait_ge(s["tok_normed"], IMAGES)
            pe.wait_ge(s["nt_copied"], IMAGES)
            pe.wait_ge(s["mixed_s"], TILES * IMAGES)
            pe.wait_ge(s["logits_done"], IMAGES)

            def hidden(i, again):
                for c in range(IC):
                    if again:
                        pe.wait_ge(s["gelu_done"], IC * i - (IC - 1 - c))
                    nc.tensor.matmul(quad[:, c, 0:TOKENS], sw1_sb[:, c * P:(c + 1) * P],
                                     normed_t_all[:, bass.ds(i * TOKENS, TOKENS)],
                                     start=True, stop=True).then_inc(s["hid_done"], 1)

            def shared(i, b, again):
                pe.wait_ge(s["gelu_done"], IC * i + IC)
                if again:
                    pe.wait_ge(s["base_done"], TILES * i - TILES)
                for t in range(TILES):
                    for c in range(IC):
                        mm = nc.tensor.matmul(bank[b][0:WIDTH[t], t * P:(t + 1) * P],
                                              gelu_sb[:, b, c, START[t]:START[t] + WIDTH[t]],
                                              sw2_sb[:, c, :], start=(c == 0), stop=(c == IC - 1))
                mm.then_inc(s["shared_done"], 1)

            hidden(0, False)

            def route():
                pe.wait_ge(s["onehot_s"], 1)
                flat = onehot[:, :, :].rearrange("p t e -> p (t e)")
                nc.tensor.matmul(bank[2][:, 0:ALL_TILES * EXPERTS], const("before"), flat, start=True, stop=True)
                nc.tensor.matmul(bank[3][:, 0:ALL_TILES * EXPERTS], const("ones"), flat,
                                 start=True, stop=True).then_inc(s["rank_done"], 1)
            hidden(1, True)
            shared(0, 0, False)
            route()
            hidden(2, True)
            shared(1, 1, False)
            with pe.Fori(1, IMAGES // 2 - 1) as m:
                hidden(2 * m + 1, True)
                shared(2 * m, 0, True)
                hidden(2 * m + 2, True)
                shared(2 * m + 1, 1, True)
            hidden(IMAGES - 1, True)
            shared(IMAGES - 2, 0, True)
            shared(IMAGES - 1, 1, True)

            pe.wait_ge(s["expert_in"], 48)
            pe.wait_ge(s["expert_of_tile_s"], 1)
            pe.wait_ge(s["base_done"], ALL_TILES)
            pe.wait_ge(s["pos_done"], 1)

            def row_transpose(m, off, b, again):
                pe.wait_ge(row_in[off % 4], 16 * (m + off // 4) + 16)
                if again:
                    pe.wait_ge(s["row_t_copied"], 4 * m + off)
                nc.tensor.transpose(row_t_ps, row_c[:, off % 4, 0:P],
                                    ident).then_inc(s["row_t_done"], 1)

            def up(j, b, again):
                e = pe.value_load(expert_of_tile[0:1, bass.ds(j, 1)], min_val=0, max_val=EXPERTS - 1)
                pe.wait_ge(s["row_t_copied"], j + 1)
                if again:
                    pe.wait_ge(s["silu_done"], j - 1)
                nc.tensor.matmul(silu_ps[b], row_t[:, b, :], w1_sb[:, bass.ds(e * INNER, INNER)],
                                 start=True, stop=True).then_inc(s["up_done"], 1)
                if again:
                    pe.wait_ge(s["gated_s"], j - 1)
                nc.tensor.matmul(gate_ps_c[b], row_t[:, b, :], w3_sb[:, bass.ds(e * INNER, INNER)],
                                 start=True, stop=True).then_inc(s["up_done"], 1)

            def gated_transpose(j, b, again):
                pe.wait_ge(s["gated_s"], j + 1)
                if again:
                    pe.wait_ge(s["gt_copied"], j)
                for c in range(IC):
                    mm = nc.tensor.transpose(gated_t_ps[:, c * P:(c + 1) * P],
                                             gated[:, b, c * P:(c + 1) * P], ident)
                mm.then_inc(s["gt_done"], 1)

            def down(j, b, again):
                e = pe.value_load(expert_of_tile[0:1, bass.ds(j, 1)], min_val=0, max_val=EXPERTS - 1)
                pe.wait_ge(s["gt_copied"], j + 1)
                if again:
                    pe.wait_ge(s["fin_done"], j - 1)
                for c in range(IC):
                    mm = nc.tensor.matmul(down_ps[b], gated_t[:, b, c * P:(c + 1) * P],
                                          w2_sb[:, bass.ds(e * INNER + c * P, P)],
                                          start=(c == 0), stop=(c == IC - 1))
                mm.then_inc(s["down_done"], 1)

            def tile_step(m, off, again, rows_ahead, up_ahead):
                j, b = 4 * m + off, off % 2
                if rows_ahead:
                    row_transpose(m, off + 2, b, True)
                gated_transpose(j, b, again or off > 0)
                if up_ahead:
                    up(j + 1, 1 - b, again or off > 0)
                down(j, b, again)

            row_transpose(0, 0, 0, False)
            row_transpose(0, 1, 1, True)
            up(0, 0, False)
            for off in range(4):
                tile_step(0, off, off > 1, True, True)
            with pe.Fori(1, SLOT_TILES // 4 - 1) as m:
                for off in range(4):
                    tile_step(m, off, True, True, True)
            for off in range(4):
                tile_step(SLOT_TILES // 4 - 1, off, True, off < 2, off < 3)

        @block.vector
        def _(dve):
            def norm_stats(name, k, im, tiles, width, src):
                settle(dve)
                for t in range(tiles):
                    ins = nc.vector.bn_stats(out=stats[0:width, k, t, :], in_=src(t))
                ins.then_inc(s[name + "_stat"], 1)
                dve.wait_ge(s[name + "_stat"], value(im, 1, 1))
                settle(dve)
                for t in range(tiles):
                    ins = nc.vector.bn_aggr(out=meanvar[0:width, k, t, :], in_=stats[0:width, k, t, :])
                ins.then_inc(s[name + "_meanvar"], 1)
                dve.wait_ge(s[name + "_meanvar"], value(im, 1, 1))

            def norm_apply(k, tiles, width, src, dst, power, done_sem):
                for t in range(tiles):
                    ins = nc.vector.tensor_scalar(dst(t), src(t), meanvar[0:width, k, t, 0:1],
                                                  power[0:width, t:t + 1], ALU.subtract, ALU.mult)
                ins.then_inc(s[done_sem], 1)

            def residual_rows(which):
                return lambda t: rows[:, bass.ds(number(which) * TILES + t, 1), P:2 * P].rearrange("p o c -> p (o c)")

            def powers(now, k_free):
                def link(k, ins):
                    ins.then_inc(s["newton"], 1)
                    dve.wait_ge(s["newton"], value(now, NEWTON, k))
                bits = guess[:, :].bitcast(I32)
                link(1, nc.vector.tensor_scalar(bits, var_sb[:, :].bitcast(I32), 1, None,
                                                ALU.logical_shift_right))
                yield
                link(2, nc.vector.tensor_scalar(bits, bits, -1.0, float(0x5f3759df), ALU.mult, ALU.add))
                yield
                for n in range(3):
                    link(3 * n + 3, nc.vector.tensor_tensor(square[:, :], guess[:, :], guess[:, :], ALU.mult))
                    yield
                    link(3 * n + 4, nc.vector.scalar_tensor_tensor(
                        out=square[:, :], in0=square[:, :], scalar=-0.5, in1=var_sb[:, :],
                        op0=ALU.mult, op1=ALU.mult))
                    yield
                    if n == 2:
                        k_free()
                    link(3 * n + 5, nc.vector.scalar_tensor_tensor(
                        out=(rstd if n == 2 else guess)[:, :], in0=square[:, :], scalar=1.5, in1=guess[:, :],
                        op0=ALU.add, op1=ALU.mult))
                    yield

            def step(st):
                ia, iq, is_, il, ig = (st.get(n) for n in "AQSLG")
                now = st["step"]
                if il:
                    if first(il, 1):
                        dve.wait_ge(s["xin_init"], 1)
                    dve.wait_ge(s["mixed_s"], value(il, TILES, TILES))
                    mine = rows[:, bass.ds(number(il) * TILES, TILES), P:2 * P]
                    nc.vector.scalar_tensor_tensor(out=mine, in0=mixed[:, :, :], scalar=0.0, in1=mine,
                                                   op0=ALU.max, op1=ALU.add).then_inc(s["h2_done"], 1)
                    dve.wait_ge(s["h2_done"], value(il, 1, 1))
                    norm_stats("ln2", 2, il, TILES, P, residual_rows(il))
                if iq:
                    bq = parity(iq)

                def rotate(t):
                    dve.wait_ge(s["qkv_done"], value(iq, TILES, t + 1))
                    if t > 1 or not first(iq, 1):
                        dve.wait_ge(s["qk_done"], value(iq, TILES, t - 1))
                    both = qkv_ps[:, 0:2 * P].rearrange("p (a c) -> p a c", a=2)
                    pairs = qkv_ps[:, 0:2 * P].rearrange("p (a c two) -> p a c two", a=2, two=2)
                    cos = const("cos")[:, t * P:(t + 1) * P]
                    sin = const("sin")[:, t * P:(t + 1) * P]
                    nc.vector.tensor_tensor(rot_a[:, t % 2, :, :], both,
                                            cos.unsqueeze(1).broadcast_to([P, 2, P]),
                                            ALU.mult).then_inc(s["rot_done"], 1)
                    nc.vector.tensor_tensor(
                        rot_b[:, t % 2, :, :].rearrange("p a (c two) -> p a c two", two=2),
                        pairs[:, :, :, ::-1],
                        sin.rearrange("p (c two) -> p c two", two=2).unsqueeze(1)
                        .broadcast_to([P, 2, P // 2, 2]),
                        ALU.mult).then_inc(s["rot_done"], 1)

                def mask(t):
                    w = WIDTH[t]
                    dve.wait_ge(s["scores_done"], value(is_, TILES, t + 1))
                    if t > 1 or not first(is_, 1):
                        dve.wait_ge(s["mix_done"], value(is_, TILES, t - 1 if t > 1 else 0))
                    nc.vector.tensor_tensor(
                        probs[0:w, t % 2, :, 0:w].rearrange("p (g e) n -> p g e n", g=2), score_ps(t),
                        const("causal")[0:w, 0:w].unsqueeze(1).unsqueeze(1).broadcast_to([w, 2, 4, w]),
                        ALU.mult).then_inc(s["probs_done"], 1)

                def residual(t):
                    w = WIDTH[t]
                    dve.wait_ge(s["back_done"], value(is_, TILES, t + 1))
                    nc.vector.scalar_tensor_tensor(
                        out=mixed[0:w, t, :], in0=back_ps[0:w, :], scalar=const("gamma_pos")[0:w, t:t + 1],
                        in1=xin[0:w, parity(is_), t, :], op0=ALU.mult, op1=ALU.add).then_inc(s["mixed_s"], 1)

                if is_:
                    dve.wait_ge(s["state_done"], value(is_, 1, 1))
                    if not first(is_, 1):
                        dve.wait_ge(s["mix_done"], value(is_, TILES, 0))
                    nc.vector.tensor_tensor(state[:, :, :], state_ps.rearrange("p (a c) -> p a c", a=2),
                                            const("block_diag").unsqueeze(1).broadcast_to([P, 2, P]),
                                            ALU.mult).then_inc(s["state_masked"], 1)
                if iq:
                    rotate(0)
                if ia:
                    dve.wait_ge(s["tok_done"], value(ia, 1, 1))
                    norm_stats("tok", 0, ia, 2, HALF, lambda t: tok_ps[0:HALF, t, :])
                    if not first(ia, 1):
                        dve.wait_ge(s["tok_rstd_s"], value(ia, 1, 0))
                    nc.vector.tensor_scalar(tok_var[0:HALF, :], meanvar[0:HALF, 0, 0:2, 1],
                                            EPS, None, ALU.add).then_inc(s["tok_vareps"], 1)
                if iq:
                    rotate(1)
                if is_:
                    mask(0)
                if ia:
                    dve.wait_ge(s["tok_rstd_s"], value(ia, 1, 1))
                    if not first(ia, 1):
                        dve.wait_ge(s["tok_scaled_s"], value(ia, 1, 0))
                    norm_apply(0, 2, HALF, lambda t: tok_ps[0:HALF, t, :], lambda t: tok_norm[0:HALF, t, :],
                               tok_rstd, "tok_normed")
                if is_:
                    mask(1)
                if iq:
                    rotate(2)
                if ig:
                    dve.wait_ge(s["gate_done"], value(ig, 1, 1))
                    nc.vector.tensor_copy(logits[:, bass.ds(number(ig) * TILES, TILES), :],
                                          gate_ps.rearrange("p (t e) -> p t e", e=EXPERTS)
                                          ).then_inc(s["logits_done"], 1)
                if iq:
                    kk = qk[:, bq, 1, :, :].rearrange("p t (g d) -> p (t g) d", d=HD)
                    dve.wait_ge(s["qk_done"], value(iq, TILES, TILES))
                    nc.vector.tensor_reduce(gn_sum[:, :], kk, AX_X, ALU.add).then_inc(s["gn_sum_s"], 1)
                    dve.wait_ge(s["gn_sum_s"], value(iq, 1, 1))
                    nc.vector.tensor_scalar(gn_mean[:, :], gn_sum[:, :], 1.0 / HD, None,
                                            ALU.mult).then_inc(s["gn_mean_s"], 1)
                if ia:
                    dve.wait_ge(s["h_done"], value(ia, 1, 1))
                    if first(ia, 1):
                        dve.wait_ge(s["txt_in"], 16)
                        dve.wait_ge(s["pad_made"], 3)
                    norm_stats("ln1", 1, ia, TILES, P, residual_rows(ia))
                if is_:
                    mask(2)
                nc.vector.tensor_scalar(var_sb[:, 0:2 * TILES].rearrange("p (k t) -> p k t", k=2),
                                        meanvar[:, 1:3, :, 1], EPS, None, ALU.add).then_inc(s["norm_vars"], 1)
                if iq:
                    dve.wait_ge(s["gn_sq_s"], value(iq, 1, 1))
                    nc.vector.tensor_reduce(gn_var[:, :], gn_sq[:, :].rearrange("p (g d) -> p g d", d=HD),
                                            AX_X, ALU.add).then_inc(s["gn_var_s"], 1)
                    dve.wait_ge(s["gn_var_s"], value(iq, 1, 1))
                nc.vector.tensor_scalar(var_sb[:, 2 * TILES:NORMS], gn_var[:, :], 1.0 / HD, EPS,
                                        ALU.mult, ALU.add).then_inc(s["norm_vars"], 1)
                dve.wait_ge(s["norm_vars"], value(now, 2, 2))

                def k_free():
                    if iq and not first(iq, 1):
                        dve.wait_ge(s["k_norm_s"], value(iq, 1, 0))
                    elif type(now[0]) is int and now[1] > IMAGES:
                        dve.wait_ge(s["k_norm_s"], IMAGES)
                newton = powers(now, k_free)
                for _ in range(4):
                    next(newton)
                if is_:
                    residual(0)
                for _ in range(7):
                    next(newton)
                if is_:
                    residual(1)
                if ia:
                    if not first(ia, 2):
                        dve.wait_ge(s["xt_done"], value(ia, 1, -1))
                if is_:
                    residual(2)
                if ia:
                    if is_:
                        dve.wait_ge(s["mixed_s"], value(is_, TILES, TILES))
                    norm_apply(1, TILES, P, residual_rows(ia), lambda t: xin[:, parity(ia), t, :],
                               rstd[:, 0:TILES], "xin_done")
                if il:
                    if not first(il, 2):
                        dve.wait_ge(s["nt_done"], value(il, 1, -1))
                        dve.wait_ge(norm_moved[parity(il)], 48 * half_number(il))
                    norm_apply(2, TILES, P, residual_rows(il), lambda t: normed[:, parity(il), t, :],
                               rstd[:, TILES:2 * TILES], "normed_s")

            nc.vector.memset(near_sb[:, :, :, :], 0.0).then_inc(s["grid_init"], 1)
            dve.wait_ge(s["par_in"], 16)
            dve.wait_ge(s["const_in"], 16)
            dve.wait_ge(s["grid_init"], 1)
            flat = near_sb[:, :, :, :].rearrange("p a i j -> p (a i j)")
            nc.vector.tensor_scalar(flat, flat, par("near_bias"), None, ALU.add).then_inc(s["grid_init"], 1)
            nc.vector.memset(meanvar[:, :, :, :], 1.0).then_inc(s["grid_init"], 1)
            nc.vector.memset(gn_var[:, :], 1.0).then_inc(s["grid_init"], 1)
            dve.wait_ge(s["grid_init"], 4)
            run_images(dve, step)

            done = [0]

            def link(ins):
                done[0] += 1
                ins.then_inc(s["route_step"], 1)
                dve.wait_ge(s["route_step"], done[0])

            def over_experts(ap):
                return ap.unsqueeze(2).broadcast_to([ap.shape[0], ap.shape[1], EXPERTS])

            dve.wait_ge(s["logits_done"], IMAGES)
            link(nc.vector.tensor_reduce(rt_m[:, :], logits[:, :, :], AX_X, ALU.max))
            link(nc.vector.tensor_tensor(rt_eq[:, :, :], logits[:, :, :], over_experts(rt_m[:, :]), ALU.is_equal))
            link(nc.vector.tensor_tensor(rt_cand[:, :, :], rt_eq[:, :, :],
                                         const("descending").unsqueeze(1).broadcast_to([P, ALL_TILES, EXPERTS]),
                                         ALU.mult))
            link(nc.vector.tensor_reduce(rt_best[:, :], rt_cand[:, :, :], AX_X, ALU.max))
            link(nc.vector.tensor_tensor(rt_hit[:, :, :], rt_cand[:, :, :], over_experts(rt_best[:, :]), ALU.is_equal))
            nc.vector.tensor_tensor(
                onehot[:, :, :].rearrange("p (b t) e -> p b t e", t=TILES),
                rt_hit[:, :, :].rearrange("p (b t) e -> p b t e", t=TILES),
                over_experts(const("valid")).unsqueeze(1).broadcast_to([P, IMAGES, TILES, EXPERTS]),
                ALU.mult).then_inc(s["onehot_s"], 1)
            link(nc.vector.memset(rt_zero[:, :], 0.0))
            dve.wait_ge(s["rank_done"], 1)
            link(nc.vector.tensor_copy(rt_tot[:, :, :],
                                       bank[3][:, 0:ALL_TILES * EXPERTS].rearrange("p (t e) -> p e t", e=EXPERTS)))
            link(nc.vector.tensor_tensor_scan(rt_cum[:, :, :].rearrange("p e t -> p (e t)"),
                                              rt_tot[:, :, :].rearrange("p e t -> p (e t)"), rt_zero[:, :],
                                              0.0, ALU.add, ALU.add))
            link(nc.vector.tensor_tensor(rt_exc[:, :, :], rt_cum[:, :, :], rt_tot[:, :, :], ALU.subtract))
            link(nc.vector.tensor_reduce(rt_n[:, :], rt_tot[:, :, :], AX_X, ALU.add))
            link(nc.vector.tensor_scalar(rt_int[:, :], rt_n[:, :], float(P - 1), None, ALU.add))
            link(nc.vector.tensor_scalar(rt_mod[:, :], rt_int[:, :], -P, None, ALU.bitwise_and))
            link(nc.vector.tensor_copy(rt_pad[:, :], rt_mod[:, :]))
            link(nc.vector.tensor_tensor_scan(rt_end[:, :], rt_pad[:, :], rt_zero[:, 0:EXPERTS],
                                              0.0, ALU.add, ALU.add))
            link(nc.vector.tensor_tensor(rt_off[:, :], rt_end[:, :], rt_pad[:, :], ALU.subtract))
            link(nc.vector.tensor_tensor(rt_off2[:, :], rt_off[:, :], rt_exc[:, :, 0], ALU.subtract))
            link(nc.vector.tensor_tensor(rt_base[:, :, :], rt_exc[:, :, :],
                                         rt_off2[:, :].unsqueeze(2).broadcast_to([P, EXPERTS, ALL_TILES]), ALU.add))
            link(nc.vector.tensor_tensor(rt_pos[:, :, :],
                                         bank[2][:, 0:ALL_TILES * EXPERTS].rearrange("p (t e) -> p t e", e=EXPERTS),
                                         rt_base[:, :, :].rearrange("p e t -> p t e"), ALU.add))
            link(nc.vector.tensor_tensor(rt_eq[:, :, :], rt_pos[:, :, :], onehot[:, :, :], ALU.mult))
            link(nc.vector.tensor_reduce(rt_posf[:, :], rt_eq[:, :, :], AX_X, ALU.add))
            nc.vector.tensor_copy(slot_of[:, :], rt_posf[:, :]).then_inc(s["pos_done"], 1)
            link(nc.vector.tensor_tensor(rt_ge[:, :, :], over_experts(const("tile_start")),
                                         rt_end[:, :].unsqueeze(1).broadcast_to([P, SLOT_TILES, EXPERTS]), ALU.is_ge))
            link(nc.vector.tensor_reduce(rt_te[:, :], rt_ge[:, :, :], AX_X, ALU.add))
            nc.vector.tensor_scalar(expert_of_tile[:, :], rt_te[:, :], float(EXPERTS - 1), None,
                                    ALU.min).then_inc(s["expert_of_tile_s"], 1)

            with dve.Fori(0, IMAGES // 2) as m:
                for b in range(2):
                    dve.wait_ge(s["shared_done"], 2 * m + (b + 1))
                    for t in range(TILES):
                        w = WIDTH[t]
                        mine = rows[0:w, bass.ds((2 * m + b) * TILES + t, 1), P:2 * P].rearrange("p o c -> p (o c)")
                        nc.vector.tensor_tensor(mine, bank[b][0:w, t * P:(t + 1) * P], mine,
                                                ALU.add).then_inc(s["base_done"], 1)

            def gate(j, b, again):
                dve.wait_ge(s["silu_done"], j + 1)
                dve.wait_ge(s["up_done"], 2 * j + 2)
                if again:
                    dve.wait_ge(s["gt_done"], j - 1)
                nc.vector.tensor_tensor(gated[:, b, :], silu_c[:, b, :], gate_ps_c[b], ALU.mult).then_inc(s["gated_s"], 1)

            def finish(m, off, again):
                dve.wait_ge(s["down_done"], 4 * m + (off + 1))
                if again:
                    dve.wait_ge(out_sent[off], 16 * m)
                b = off % 2
                nc.vector.tensor_tensor(fin_c[:, off, :], down_ps[b],
                                        row_c[:, off, P:2 * P], ALU.add).then_inc(s["fin_done"], 1)

            gate(0, 0, False)
            for off in range(4):
                gate(off + 1, (off + 1) % 2, off > 0)
                finish(0, off, False)
            with dve.Fori(1, SLOT_TILES // 4 - 1) as m:
                for off in range(4):
                    gate(4 * m + (off + 1), (off + 1) % 2, True)
                    finish(m, off, True)
            for off in range(4):
                if off < 3:
                    gate(SLOT_TILES - 4 + off + 1, (off + 1) % 2, True)
                finish(SLOT_TILES // 4 - 1, off, True)


def constants():
    f = np.float32
    c = np.zeros((P, CONST_COLS), f)

    def put(name, a):
        lo, hi = CONST_AT[name]
        c[:, lo:hi] = a
    i = np.arange(P)
    put("identity", np.eye(P))
    put("causal", i[None, :] >= i[:, None])
    put("block_diag", i[:, None] // HD == i[None, :] // HD)
    put("before", i[:, None] < i[None, :])
    put("ones", 1.0)
    same = np.zeros((P, P), f)
    same[:64, :64] = np.eye(64)
    eye = np.eye(HD)
    A, AY, B, BY = 64, 80, 96, 112
    for src, dst in ((A, 64), (B, 80), (AY, 96), (BY, 112)):
        same[src:src + HD, dst:dst + HD] = eye
    put("select_same", same)
    near = np.zeros((P, 4 * HD), f)
    for n, src in enumerate((B, A, BY - 64, AY - 64)):
        near[src:src + HD, n * HD:(n + 1) * HD] = eye
    put("select_neighbours", near)
    half = P // 2
    scale_vec = (np.arange(0, P, 2, dtype=f) + f(0.4 * P)) / f(1.4 * P)
    s = np.arange(TOKENS, dtype=f)
    scale = scale_vec[None, :] ** (s / f(512.0))[:, None]
    inv_freq = f(1.0) / f(10000.0) ** (np.arange(half, dtype=f) / f(half))
    angle = s[:, None] * inv_freq[None, :]
    sin = np.repeat(np.sin(angle) * scale, 2, axis=-1)
    cos = np.repeat(np.cos(angle) * scale, 2, axis=-1)
    sin[:, 0::2] *= -1
    for t in range(TILES):
        w, a = WIDTH[t], START[t]
        for name, table in (("cos", cos), ("sin", sin)):
            lo = CONST_AT[name][0] + t * P
            c[:w, lo:lo + P] = table[a:a + w]
        pos = np.arange(a, a + w, dtype=np.float64)
        c[:w, CONST_AT["gamma_neg"][0] + t] = GAMMA ** -pos
        c[:w, CONST_AT["gamma_pos"][0] + t] = GAMMA ** pos
        c[:w, CONST_AT["valid"][0] + t] = 1.0
    put("head_of_four", i[:, None] % 64 // HD == np.arange(4)[None, :])
    put("descending", EXPERTS - np.arange(EXPERTS)[None, :])
    put("minus_half", -0.5)
    put("tile_start", P * np.arange(SLOT_TILES)[None, :])
    return c


def lay_out(inp):
    x = inp["x"].reshape(IMAGES, 3, GRID, 16, GRID, 16).transpose(0, 1, 3, 5, 2, 4)
    x = x.reshape(IMAGES, KC, P, PATCHES).transpose(0, 2, 1, 3)
    zero = np.zeros((HD, 3, 8, 16), np.float32)
    sx = inp["L0_tok_W_sx"].reshape(HD, 3, 16, 16)
    sy = inp["L0_tok_W_sy"].reshape(HD, 3, 16, 16)
    zx = zero.transpose(0, 1, 3, 2)
    a = np.concatenate([zx, sx[..., :8]], axis=3)
    b = np.concatenate([sx[..., 8:], zx], axis=3)
    ay = np.concatenate([zero, sy[:, :, :8]], axis=2)
    by = np.concatenate([sy[:, :, 8:], zero], axis=2)
    w = np.concatenate([inp["L0_tok_W_main"]] + [m.reshape(HD, 768) for m in (a, ay, b, by)])
    params = np.zeros((P, PAR_COLS), np.float32)
    params[:, 0] = np.concatenate([inp["L0_tok_b_main"], inp["L0_tok_b_sx"], inp["L0_tok_b_sy"],
                                   np.zeros(2 * HD, np.float32)])
    params[:, 1] = np.concatenate([params[64:, 0], params[64:, 0]])
    for name, key in (("ln_g", "L0_tok_ln_g"), ("ln_b", "L0_tok_ln_b"),
                      ("gn_w", "L0_attn_gn_weight"), ("gn_b", "L0_attn_gn_bias")):
        lo, hi = PAR_AT[name]
        params[:, lo:hi] = inp[key][None, :]
    lo, hi = PAR_AT["gate"]
    params[:, lo:hi] = inp["L0_ffn_gate_w"].T
    return {
        "x": x,
        "txt": inp["txt"],
        "patch_w": w.T.reshape(KC, P, P).transpose(1, 0, 2),
        "params": params,
        "w_qkv": np.concatenate([inp["L0_attn_Wq"], inp["L0_attn_Wk"], inp["L0_attn_Wv"]], axis=1),
        "w1": inp["L0_ffn_w1"].transpose(2, 0, 1).reshape(P, EXPERTS * INNER),
        "w3": inp["L0_ffn_w3"].transpose(2, 0, 1).reshape(P, EXPERTS * INNER),
        "w2": inp["L0_ffn_w2"].reshape(EXPERTS, P, IC, P).transpose(3, 0, 2, 1).reshape(P, EXPERTS * INNER),
        "sw1": inp["L0_ffn_sw1"].T,
        "sw2": inp["L0_ffn_sw2"].reshape(P, IC, P).transpose(2, 1, 0),
        "consts": constants(),
    }


def kernel(**inputs):
    import concourse.bacc as bacc
    from concourse.bass_utils import run_bass_kernel_spmd

    nc = bacc.Bacc("TRN2", target_bir_lowering=False, num_devices=1)
    arrays, args = {}, []
    for name, a in lay_out({k: np.asarray(v) for k, v in inputs.items()}).items():
        a = np.ascontiguousarray(a)
        arrays[f"in_{name}"] = a
        args.append(nc.dram_tensor(f"in_{name}", a.shape, mybir.dt.from_np(a.dtype), kind="ExternalInput").ap())
    args.append(nc.dram_tensor("out", (IMAGES, TOKENS, P), F32, kind="ExternalOutput").ap())
    build(nc, *args)
    r = run_bass_kernel_spmd(nc, [arrays], core_ids=[0])
    return r.results[0]["out"]
```

```python
from contextlib import ExitStack

import numpy as np
import concourse.bass as bass
from concourse import mybir

F32 = mybir.dt.float32
I32 = mybir.dt.int32
U32 = mybir.dt.uint32
ALU = mybir.AluOpType
ACT = mybir.ActivationFunctionType
AX_X = mybir.AxisListType.X

P = 128
IMAGES = 16
GRID = 14
PATCHES = GRID * GRID
TEXT = 128
TOKENS = PATCHES + TEXT
HALF = PATCHES // 2
TILES = 3
WIDTH = (HALF, HALF, TEXT)
START = (0, HALF, PATCHES)
KC = 6
HEADS = 8
HD = P // HEADS
GAMMA = 0.9
EPS = 1e-5
EXPERTS = 8
INNER = 512
IC = INNER // P
ALL_TILES = IMAGES * TILES
ALL_TOKENS = IMAGES * TOKENS
SLOT_TILES = (ALL_TOKENS + EXPERTS * (P - 1)) // P
SLOTS = SLOT_TILES * P
REST_PARTS = ((0, 4), (4, SLOT_TILES))
ROW = 260
ROW_ID = 2 * P
PAD_ID = 1 << 20

CONST_LAYOUT = [
    ("identity", P), ("causal", P), ("block_diag", P), ("before", P), ("ones", P),
    ("select_same", P), ("select_neighbours", 4 * HD), ("cos", TILES * P), ("sin", TILES * P),
    ("gamma_neg", TILES), ("gamma_pos", TILES), ("head_of_four", 4),
    ("descending", EXPERTS), ("valid", TILES), ("tile_start", SLOT_TILES),
    ("minus_half", 2),
]
CONST_AT = {}
_at = 0
for _name, _n in CONST_LAYOUT:
    CONST_AT[_name] = (_at, _at + _n)
    _at += _n
CONST_COLS = _at
PAR_LAYOUT = [("patch_bias", 1), ("near_bias", 1), ("ln_g", P), ("ln_b", P), ("gn_w", P), ("gn_b", P), ("gate", EXPERTS)]
PAR_AT = {}
_at = 0
for _name, _n in PAR_LAYOUT:
    PAR_AT[_name] = (_at, _at + _n)
    _at += _n
PAR_COLS = _at


def build(nc, x, txt, patch_w, params, w_qkv, w1, w3, w2, sw1, sw2, consts, out):
    ctx = ExitStack()
    with ctx:
        def sb(name, shape, dt=F32):
            return ctx.enter_context(nc.sbuf_tensor(name, shape, dt))

        def ps(name, shape):
            return ctx.enter_context(nc.psum_tensor(name, shape, F32))

        def sem(name):
            return ctx.enter_context(nc.semaphore(name))

        sorted_rows = nc.dram_tensor("sorted_rows", [SLOTS, ROW], F32, kind="Internal").ap()
        out_rows = out.rearrange("b t d -> (b t) d")

        const_sb = sb("const_sb", [P, CONST_COLS])

        def const(name):
            a, b = CONST_AT[name]
            return const_sb[:, a:b]

        par_sb = sb("par_sb", [P, PAR_COLS])

        def par(name):
            a, b = PAR_AT[name]
            return par_sb[:, a:b]

        patch_w_sb = sb("patch_w_sb", [P, KC, P])
        qkv_w_sb = sb("qkv_w_sb", [P, 3 * P])
        w1_sb = sb("w1_sb", [P, EXPERTS * INNER])
        w3_sb = sb("w3_sb", [P, EXPERTS * INNER])
        w2_sb = sb("w2_sb", [P, EXPERTS * INNER])
        sw1_sb = sb("sw1_sb", [P, INNER])
        sw2_sb = sb("sw2_sb", [P, IC, P])
        rows = sb("rows", [P, ALL_TILES, ROW])
        normed_t_all = sb("normed_t_all", [P, ALL_TOKENS])
        pad_row = sb("pad_row", [P, ROW])

        x_sb = sb("x_sb", [P, 2, KC, PATCHES])
        grid_sb = sb("grid_sb", [P, 2, PATCHES])
        near_sb = sb("near_sb", [P, 2, GRID, GRID])
        tok_norm = sb("tok_norm", [P, 2, P])
        tok_scaled = sb("tok_scaled", [P, 2, P])
        token_buf = sb("token_buf", [P, 4 * TILES * P])
        token_view = token_buf[:, :].rearrange("p (k b t n) -> p k b t n", k=2, b=2, t=TILES)
        xin = token_view[:, 0, :, :, :]
        normed = token_view[:, 1, :, :, :]
        xin_t = sb("xin_t", [P, TILES, P])
        rot_a = sb("rot_a", [P, 2, 2, P])
        rot_b = sb("rot_b", [P, 2, 2, P])
        qk = sb("qk", [P, 2, 2, TILES, P])
        v_pad = sb("v_pad", [P, 2, TILES, HEADS, 2 * HD])
        gn_sum = sb("gn_sum", [P, TILES * HEADS])
        gn_mean = sb("gn_mean", [P, TILES * HEADS])
        gn_sq = sb("gn_sq", [P, TILES * P])
        gn_var = sb("gn_var", [P, TILES * HEADS])
        k_cent = sb("k_cent", [P, TILES, P])
        q_t = sb("q_t", [P, TILES, P])
        k_t = sb("k_t", [P, TILES, P])
        state = sb("state", [P, 2, P])
        work = sb("work", [P, 2 * HEADS * P + 4 * TILES * P])
        probs = work[:, 0:2 * HEADS * P].rearrange("p (b h n) -> p b h n", b=2, h=HEADS)
        q_four = work[:, 2 * HEADS * P:].rearrange("p (t e n) -> p t e n", t=TILES, e=4)
        mix_t = sb("mix_t", [P, 2, P])
        mixed = sb("mixed", [P, TILES, P])
        normed_t = sb("normed_t", [P, TILES, P])
        stats = sb("stats", [P, 3, TILES, 6])
        meanvar = sb("meanvar", [P, 3, TILES, 2])
        tok_var = sb("tok_var", [P, 2])
        tok_rstd = sb("tok_rstd", [P, 2])
        NORMS = 2 * TILES + TILES * HEADS
        var_sb = sb("var_sb", [P, NORMS])
        guess = sb("guess", [P, NORMS])
        square = sb("square", [P, NORMS])
        rstd = sb("rstd", [P, NORMS])
        shift = sb("shift", [P, 2, TILES])
        logits = sb("logits", [P, ALL_TILES, EXPERTS])

        gelu_sb = work[:, 0:2 * IC * TOKENS].rearrange("p (b c n) -> p b c n", b=2, c=IC)
        qk_flat = qk[:, :, :, :, :].rearrange("p b a t n -> p (b a t n)")
        row_c = token_buf[:, 4 * (P + 4):4 * (P + 4) + 4 * P].rearrange("p (b c) -> p b c", b=4)
        fin_c = token_buf[:, 0:4 * (P + 1)].rearrange("p (b n) -> p b n", b=4)
        row_t = sb("row_t", [P, 2, P])
        x_flat = x_sb[:, :, :, :].rearrange("p b k n -> p (b k n)")
        silu_c = x_flat[:, 0:2 * INNER].rearrange("p (b n) -> p b n", b=2)
        gated = x_flat[:, 2 * INNER:4 * INNER].rearrange("p (b n) -> p b n", b=2)
        gated_t = qk_flat[:, 0:2 * INNER].rearrange("p (b n) -> p b n", b=2)
        v_flat = v_pad[:, :, :, :, :].rearrange("p b t h c -> p (b t h c)")
        TABLE = ALL_TILES * EXPERTS
        rt_m = sb("rt_m", [P, ALL_TILES])
        rt_eq = k_cent[:, :, :].rearrange("p t c -> p (t c)") \
            .rearrange("p (t e) -> p t e", e=EXPERTS)
        rt_cand = v_flat[:, 0:TABLE].rearrange("p (t e) -> p t e", e=EXPERTS)
        rt_best = sb("rt_best", [P, ALL_TILES])
        rt_hit = v_flat[:, TABLE:2 * TABLE].rearrange("p (t e) -> p t e", e=EXPERTS)
        onehot = sb("onehot", [P, ALL_TILES, EXPERTS])
        rt_tot = v_flat[:, 2 * TABLE:3 * TABLE].rearrange("p (e t) -> p e t", e=EXPERTS)
        rt_zero = v_flat[:, 3 * TABLE:4 * TABLE]
        rt_cum = gn_sq[:, :] \
            .rearrange("p (e t) -> p e t", e=EXPERTS)
        rt_exc = token_buf[:, 0:TABLE].rearrange("p (e t) -> p e t", e=EXPERTS)
        rt_n = sb("rt_n", [P, EXPERTS])
        rt_int = sb("rt_int", [P, EXPERTS], I32)
        rt_mod = sb("rt_mod", [P, EXPERTS], I32)
        rt_pad = sb("rt_pad", [P, EXPERTS])
        rt_end = sb("rt_end", [P, EXPERTS])
        rt_off = sb("rt_off", [P, EXPERTS])
        rt_off2 = sb("rt_off2", [P, EXPERTS])
        rt_base = token_buf[:, TABLE:2 * TABLE].rearrange("p (e t) -> p e t", e=EXPERTS)
        rt_pos = rot_a[:, :, :, :].rearrange("p a b c -> p (a b c)")[:, 0:ALL_TILES * EXPERTS] \
            .rearrange("p (t e) -> p t e", e=EXPERTS)
        rt_posf = sb("rt_posf", [P, ALL_TILES])
        slot_of = sb("slot_of", [P, ALL_TILES], I32)
        rt_ge = rot_b[:, :, :, :].rearrange("p a b c -> p (a b c)")[:, 0:SLOT_TILES * EXPERTS] \
            .rearrange("p (t e) -> p t e", e=EXPERTS)
        rt_te = gn_sq[:, 0:SLOT_TILES]
        expert_of_tile = sb("expert_of_tile", [P, SLOT_TILES], I32)

        bank = [ps(f"bank{i}", [P, 512]) for i in range(4)]
        quad = ps("quad", [P, 4, 512])
        patch_ps = bank[0][:, 0:PATCHES]
        tok_ps = bank[0][:, 256:512].rearrange("p (t c) -> p t c", t=2)
        xt_ps = bank[1][:, 0:TILES * P]
        qkv_ps = bank[2][:, 0:3 * P]
        back_ps = bank[1][:, TILES * P:4 * P]
        mix_ps = bank[3][:, 0:P]
        gate_ps = bank[3][:, P:P + TILES * EXPERTS]
        kt_ps = quad[:, 0, 0:TILES * P]
        state_ps = quad[:, 1, 0:2 * P]
        qt_ps = quad[:, 2, 0:TILES * P]

        def score_ps(t):
            w = WIDTH[t]
            a = 2 * (t % 2)
            return quad[0:w, a:a + 2, 0:4 * w].rearrange("p g (e n) -> p g e n", e=4)

        row_t_ps = bank[0][:, 0:P]
        silu_ps = [bank[1][:, :], bank[2][:, :]]
        gate_ps_c = [bank[3][:, :], quad[:, 0, :]]
        gated_t_ps = quad[:, 1, :]
        down_ps = [quad[:, 2, 0:P], quad[:, 3, 0:P]]

        names = """const_in par_in w_in qkvw_in txt_in expert_in shared_in
            pad_made pad_written rows_tail grid_init xin_init
            patch_done grid_done tok_done tok_stat tok_meanvar tok_rstd_s tok_normed tok_scaled_s h_done
            ln1_stat ln1_meanvar xin_done norm_vars ln_rstd_s shift_s k_vars newton_k mixed_init v_init xt_done xt_copied
            qkv_done rot_done v_done qk_done gn_sum_s gn_mean_s k_cent_s gn_sq_s gn_var_s tok_vareps
            k_norm_s k_scaled_s k_done
            q_turned k_turned q_four_s q_t_s k_t_s state_done state_masked scores_done probs_done mix_done mix_copied back_done mixed_s h2_done
            ln2_stat ln2_meanvar normed_s nt_done nt_copied gate_done logits_done
            route_step onehot_s rank_done pos_done settled rows_sent expert_of_tile_s
            hid_done gelu_done shared_done base_done
            row_t_done row_t_copied up_done silu_done gated_s gt_done gt_copied down_done fin_done
            """.split()
        s = {n: sem(n) for n in names}
        x_in = [sem(f"x_in{b}") for b in range(2)]
        norm_moved = [sem(f"norm_moved{b}") for b in range(2)]
        row_in = [sem(f"row_in{b}") for b in range(4)]
        rest_in = [sem(f"rest_in{b}") for b in range(len(REST_PARTS))]
        out_sent = [sem(f"out_sent{b}") for b in range(4)]

        def settle(eng):
            eng.sem_inc(s["settled"], 1)

        def number(im):
            return 2 * im[0] + im[1]

        def half_number(im):
            return im[0] + im[1] // 2

        def parity(im):
            return im[1] % 2

        def back(im, d):
            return (im[0], im[1] - d)

        def value(im, per, k):
            return 2 * per * im[0] + (per * im[1] + k)

        def first(im, d):
            return type(im[0]) is int and 2 * im[0] + im[1] < d

        STAGES = (("P", 0), ("A", 1), ("Q", 2), ("S", 3), ("L", 4), ("G", 5))
        LAST = STAGES[-1][1]
        PEELED = 6

        def rot_buf(im, t):
            return (im[1] * TILES + t) % 2

        def run_images(eng, step):
            def one(im, n=None):
                stages = {"step": im}
                for name, lag in STAGES:
                    if n is None or 0 <= n - lag < IMAGES:
                        stages[name] = back(im, lag)
                step(stages)
            for n in range(PEELED):
                one((0, n), n)
            with eng.Fori(PEELED // 2, IMAGES // 2) as m:
                one((m, 0))
                one((m, 1))
            for n in range(IMAGES, IMAGES + LAST):
                one((0, n), n)

        NEWTON = 11

        block = ctx.enter_context(nc.Block())

        @block.sync
        def _(sp):
            sp.dma_start(patch_w_sb[:, :, :], patch_w).then_inc(s["w_in"], 16)
            sp.dma_start(par_sb[:, :], params).then_inc(s["par_in"], 16)
            sp.dma_start(x_sb[:, 1, :, :], x[1]).then_inc(x_in[1], 16)
            sp.dma_start(rows[:, TILES - 1:ALL_TILES:TILES, P:2 * P],
                         txt.rearrange("b t d -> t b d")).then_inc(s["txt_in"], 16)
            sp.dma_start(qkv_w_sb[:, :], w_qkv).then_inc(s["qkvw_in"], 16)
            def load_x(im):
                sp.wait_ge(s["patch_done"], value(im, 1, 1))
                sp.dma_start(x_sb[:, parity(im), :, :],
                             x[bass.ds(number(im) + 2, 1)].rearrange("o p k n -> (o p) k n")
                             ).then_inc(x_in[parity(im)], 16)

            def move(im):
                sp.wait_ge(s["normed_s"], value(im, 1, 1))
                sp.dma_start(rows[:, bass.ds(number(im) * TILES, TILES), 0:P],
                             normed[:, parity(im), :, :]).then_inc(norm_moved[parity(im)], 16)
                sp.wait_ge(s["nt_copied"], value(im, 1, 1))
                sp.dma_start(normed_t_all[:, bass.ds(number(im) * TOKENS, 2 * HALF)]
                             .rearrange("p (t n) -> p t n", t=2),
                             normed_t[:, 0:2, 0:HALF]).then_inc(norm_moved[parity(im)], 16)
                sp.dma_start(normed_t_all[:, bass.ds(number(im) * TOKENS + 2 * HALF, TEXT)],
                             normed_t[:, 2, :]).then_inc(norm_moved[parity(im)], 16)

            load_x((0, 0))
            sp.wait_ge(s["pad_made"], 3)
            sp.dma_start(sorted_rows.rearrange("(j p) c -> p j c", p=P),
                         pad_row[:, :].unsqueeze(1).broadcast_to([P, SLOT_TILES, ROW])
                         ).then_inc(s["pad_written"], 16)
            load_x((0, 1))
            sp.dma_start(w1_sb[:, :], w1).then_inc(s["expert_in"], 16)
            load_x((0, 2))
            sp.dma_start(w3_sb[:, :], w3).then_inc(s["expert_in"], 16)
            load_x((0, 3))
            sp.dma_start(w2_sb[:, :], w2).then_inc(s["expert_in"], 16)
            sp.dma_start(sw1_sb[:, :], sw1).then_inc(s["shared_in"], 16)
            sp.dma_start(sw2_sb[:, :, :], sw2).then_inc(s["shared_in"], 16)
            with sp.Fori(2, IMAGES // 2 - 1) as m:
                for off in range(2):
                    load_x((m, off))
                    move((m, off - 4))
            for i in range(IMAGES - 6, IMAGES):
                move((0, i))

            sp.wait_ge(s["pad_written"], 16)
            sp.wait_ge(s["rows_sent"], 16 * ALL_TILES)

            def load_normed(m, off, free):
                if free:
                    sp.wait_ge(s["row_t_done"], 4 * (m - 1) + (off + 1))
                sp.dma_start(row_c[:, off, :],
                             sorted_rows[bass.ds((4 * m + off) * P, P), 0:P]).then_inc(row_in[off], 16)

            for off in range(4):
                load_normed(0, off, False)
            for part, (lo, hi) in enumerate(REST_PARTS):
                sp.dma_start(rows[:, lo:hi, P:ROW],
                             sorted_rows[lo * P:hi * P, P:ROW].rearrange("(j p) c -> p j c", p=P)
                             ).then_inc(rest_in[part], 16)
            with sp.Fori(1, SLOT_TILES // 4) as m:
                for off in range(4):
                    load_normed(m, off, True)
            for off in range(4):
                sp.wait_ge(out_sent[off], 16 * (SLOT_TILES // 4))

        @block.gpsimd
        def _(pool):
            nc.gpsimd.memset(pad_row[:, :], 0.0).then_inc(s["pad_made"], 1)
            pool.wait_ge(s["pad_made"], 1)
            nc.gpsimd.iota(pad_row[:, ROW_ID:ROW_ID + 1].bitcast(I32), pattern=[[0, 1]],
                           base=PAD_ID, channel_multiplier=1).then_inc(s["pad_made"], 1)
            nc.gpsimd.memset(rows[:, :, ROW_ID + 1:ROW], 0.0).then_inc(s["rows_tail"], 1)
            nc.gpsimd.iota(rows[:, :, ROW_ID:ROW_ID + 1].bitcast(I32)
                           .rearrange("p (b t) o -> p b t o", t=TILES),
                           pattern=[[TOKENS, IMAGES], [HALF, TILES], [0, 1]], base=0,
                           channel_multiplier=1).then_inc(s["rows_tail"], 1)
            nc.gpsimd.memset(rows[:, :, P:2 * P].rearrange("p (b t) c -> p b t c", t=TILES)
                             [:, :, 0:2, :], 0.0).then_inc(s["pad_made"], 1)
            nc.gpsimd.memset(mixed[:, :, :], 0.0).then_inc(s["xin_init"], 1)
            nc.gpsimd.memset(v_pad[:, :, :, :, :], 0.0).then_inc(s["v_init"], 1)

            def bc_tiles(ap, n):
                return ap.unsqueeze(1).broadcast_to([ap.shape[0], n, P])

            def step(st):
                if "A" in st:
                    ia = st["A"]

                def rotated(im, t):
                    pool.wait_ge(s["rot_done"], value(im, 2 * TILES, 2 * t + 2))
                    if not first(im, 2) and t == 0:
                        pool.wait_ge(s["state_done"], value(im, 1, -1))
                    nc.gpsimd.tensor_tensor(qk[:, parity(im), :, t, :], rot_a[:, rot_buf(im, t), :, :],
                                            rot_b[:, rot_buf(im, t), :, :],
                                            ALU.add).then_inc(s["qk_done"], 1)
                if "A" in st:
                    im = ia
                    pool.wait_ge(s["tok_normed"], value(im, 1, 1))
                    if first(im, 1):
                        pool.wait_ge(s["par_in"], 16)
                    nc.gpsimd.tensor_tensor(tok_scaled[0:HALF, :, :], tok_norm[0:HALF, :, :],
                                            bc_tiles(par("ln_g")[0:HALF, :], 2),
                                            ALU.mult).then_inc(s["tok_scaled_s"], 1)
                    pool.wait_ge(s["tok_scaled_s"], value(im, 1, 1))
                    if first(im, 1):
                        pool.wait_ge(s["pad_made"], 3)
                    nc.gpsimd.tensor_tensor(rows[0:HALF, bass.ds(number(im) * TILES, 2), P:2 * P],
                                            tok_scaled[0:HALF, :, :],
                                            bc_tiles(par("ln_b")[0:HALF, :], 2),
                                            ALU.add).then_inc(s["h_done"], 1)
                if "Q" in st:
                    rotated(st["Q"], 1)
                    rotated(st["Q"], 2)
                    im = st["Q"]
                    b = parity(im)
                    kk = qk[:, b, 1, :, :].rearrange("p t (g d) -> p (t g) d", d=HD)
                    cent = k_cent[:, :, :].rearrange("p t (g d) -> p (t g) d", d=HD)

                    def over_group(ap):
                        return ap.unsqueeze(2).broadcast_to([P, TILES * HEADS, HD])
                now = st["step"]
                pool.wait_ge(s["norm_vars"], value(now, 1, 1))
                if type(now[0]) is not int or now[1] > 0:
                    pool.wait_ge(s["shift_s"], value(now, 1, 0))
                past = type(now[0]) is int and now[1] > IMAGES
                if "A" in st and not first(ia, 1):
                    pool.wait_ge(s["xin_done"], value(ia, 1, 0))
                elif past:
                    pool.wait_ge(s["xin_done"], IMAGES)
                if "L" in st and not first(st["L"], 1):
                    pool.wait_ge(s["normed_s"], value(st["L"], 1, 0))
                elif past and "L" not in st:
                    pool.wait_ge(s["normed_s"], IMAGES)
                nc.gpsimd.tensor_tensor(rstd[:, 0:2 * TILES], var_sb[:, 0:2 * TILES],
                                        const("minus_half")[:, 0:1].broadcast_to([P, 2 * TILES]),
                                        ALU.pow).then_inc(s["ln_rstd_s"], 1)
                if "Q" in st:
                    pool.wait_ge(s["gn_mean_s"], value(im, 1, 1))
                    nc.gpsimd.tensor_tensor(cent, kk, over_group(gn_mean[:, :]),
                                            ALU.subtract).then_inc(s["k_cent_s"], 1)
                    pool.wait_ge(s["gn_sq_s"], value(im, 1, 1))
                    nc.gpsimd.tensor_tensor(k_cent[:, :, :], k_cent[:, :, :], bc_tiles(par("gn_w"), TILES),
                                            ALU.mult).then_inc(s["k_scaled_s"], 1)
                    pool.wait_ge(s["newton_k"], value(st["step"], NEWTON, NEWTON))
                    pool.wait_ge(s["k_scaled_s"], value(im, 1, 1))
                    nc.gpsimd.tensor_tensor(cent, cent, over_group(rstd[:, 2 * TILES:NORMS]),
                                            ALU.mult).then_inc(s["k_norm_s"], 1)
                    pool.wait_ge(s["k_norm_s"], value(im, 1, 1))
                    nc.gpsimd.tensor_tensor(qk[:, b, 1, :, :], k_cent[:, :, :], bc_tiles(par("gn_b"), TILES),
                                            ALU.add).then_inc(s["k_done"], 1)
                if "A" in st:
                    rotated(ia, 0)
                if "P" in st:
                    pool.wait_ge(s["tok_vareps"], value(st["P"], 1, 1))
                    nc.gpsimd.tensor_tensor(tok_rstd[0:HALF, :], tok_var[0:HALF, :],
                                            const("minus_half")[0:HALF, :], ALU.pow).then_inc(s["tok_rstd_s"], 1)

            pool.wait_ge(s["const_in"], 16)
            run_images(pool, step)

            pool.wait_ge(s["pos_done"], 1)
            pool.wait_ge(s["pad_written"], 16)
            pool.wait_ge(s["rows_tail"], 2)
            for b in range(2):
                pool.wait_ge(norm_moved[b], 48 * (IMAGES // 2))
            for i in range(IMAGES):
                for t in range(TILES):
                    j = TILES * i + t
                    pool.wait_ge(s["base_done"], j + 1)
                    nc.gpsimd.indirect_dma_start(
                        out=sorted_rows,
                        out_offset=bass.IndirectOffsetOnAxis(
                            ap=slot_of[0:WIDTH[t], j:j + 1].bitcast(U32), axis=0),
                        in_=rows[0:WIDTH[t], j, :], in_offset=None).then_inc(s["rows_sent"], 16)

            with pool.Fori(0, SLOT_TILES // 4) as m:
                for off in range(4):
                    pool.wait_ge(s["fin_done"], 4 * m + (off + 1))
                    settle(pool)
                    nc.gpsimd.indirect_dma_start(
                        out=out_rows,
                        out_offset=bass.IndirectOffsetOnAxis(
                            ap=fin_c[:, off, P:P + 1].bitcast(U32), axis=0),
                        in_=fin_c[:, off, 0:P],
                        in_offset=None,
                        bounds_check=ALL_TOKENS - 1, oob_is_err=False).then_inc(out_sent[off], 16)

        @block.scalar
        def _(act):
            def step(st):
                ip, ia, iq, is_, il, ig = (st.get(n) for n in "PAQSLG")

                def v_copy(im, t):
                    act.wait_ge(s["rot_done"], value(im, 2 * TILES, 2 * t + 2))
                    if not first(im, 2):
                        act.wait_ge(s["mix_done"], value(im, TILES, t + 1 - 2 * TILES))
                    mine = v_pad[:, parity(im), t, :, :].rearrange("p (r e) c -> p r (e c)", e=2) \
                        .rearrange("p r (f d) -> p r f d", d=HD)[:, :, 0::3, :]
                    nc.scalar.activation(mine, qkv_ps[:, 2 * P:3 * P].rearrange("p (r e d) -> p r e d", e=2, d=HD),
                                         ACT.Identity,
                                         scale=const("gamma_neg")[:, t:t + 1]).then_inc(s["v_done"], 1)

                def mix_copy(t):
                    w = WIDTH[t]
                    act.wait_ge(s["mix_done"], value(is_, TILES, t + 1))
                    if t > 1 or not first(is_, 1):
                        act.wait_ge(s["back_done"], value(is_, TILES, t - 1))
                    nc.scalar.activation(mix_t[:, t % 2, 0:w], mix_ps[:, 0:w],
                                         ACT.Copy).then_inc(s["mix_copied"], 1)

                if is_:
                    act.wait_ge(s["q_turned"], value(is_, 1, 1))
                    if not first(is_, 1):
                        act.wait_ge(s["mix_done"], value(is_, TILES, 0))
                    q3 = qt_ps.rearrange("p (t n) -> p t n", t=TILES)

                def silu_q(of):
                    for e in of:
                        nc.scalar.activation(q_four[:, :, e, :], q3, ACT.Silu,
                                             scale=const("head_of_four")[:, e:e + 1]).then_inc(s["q_four_s"], 1)
                if is_:
                    silu_q(range(2))
                if iq:
                    v_copy(iq, 1)
                if is_:
                    silu_q(range(2, 4))
                    act.wait_ge(s["k_turned"], value(is_, 1, 1))
                    nc.scalar.activation(k_t[:, :, :].rearrange("p t c -> p (t c)"), kt_ps,
                                         ACT.Copy).then_inc(s["k_t_s"], 1)
                    nc.scalar.activation(q_t[:, :, :], q3, ACT.Silu).then_inc(s["q_t_s"], 1)
                    if not first(is_, 1):
                        act.wait_ge(s["h2_done"], value(is_, 1, 0))
                    else:
                        act.wait_ge(s["xin_init"], 1)
                    act.wait_ge(s["xin_done"], value(is_, 1, 1))
                    nc.scalar.activation(mixed[:, :, :], xin[:, parity(is_), :, :],
                                         ACT.Copy).then_inc(s["mixed_init"], 1)
                if ig:
                    act.wait_ge(s["nt_done"], value(ig, 1, 1))
                    if not first(ig, 1):
                        act.wait_ge(s["gate_done"], value(ig, 1, 0))
                        before = back(ig, 1)
                        act.wait_ge(norm_moved[parity(before)], 48 * half_number(before) + 48)
                    nc.scalar.activation(normed_t[:, :, :].rearrange("p t c -> p (t c)"), xt_ps,
                                         ACT.Copy).then_inc(s["nt_copied"], 1)
                if iq:
                    v_copy(iq, 2)

                def norm_apply(k, im, dst, done_sem):
                    act.wait_ge(s["shift_s"], value(st["step"], 1, 1))
                    for t in range(TILES):
                        settle(act)
                        ins = nc.scalar.activation(
                            dst(t), rows[:, bass.ds(number(im) * TILES + t, 1), P:2 * P].rearrange("p o c -> p (o c)"),
                            ACT.Identity, bias=shift[:, k, t:t + 1],
                            scale=rstd[:, k * TILES + t:k * TILES + t + 1])
                    ins.then_inc(s[done_sem], 1)
                if ia:
                    if not first(ia, 2):
                        act.wait_ge(s["xt_done"], value(ia, 1, -1))
                        act.wait_ge(s["mixed_init"], value(ia, 1, -1))
                    norm_apply(0, ia, lambda t: xin[:, parity(ia), t, :], "xin_done")
                if iq:
                    act.wait_ge(s["k_cent_s"], value(iq, 1, 1))
                    if not first(iq, 1):
                        act.wait_ge(s["gn_var_s"], value(iq, 1, 0))
                    nc.scalar.activation(gn_sq[:, :], k_cent[:, :, :].rearrange("p t c -> p (t c)"),
                                         ACT.Square).then_inc(s["gn_sq_s"], 1)
                if is_:
                    mix_copy(0)
                if ia:
                    act.wait_ge(s["xt_done"], value(ia, 1, 1))
                    if not first(ia, 1):
                        act.wait_ge(s["qkv_done"], value(ia, TILES, 0))
                    nc.scalar.activation(xin_t[:, :, :].rearrange("p t c -> p (t c)"), xt_ps,
                                         ACT.Copy).then_inc(s["xt_copied"], 1)
                if is_:
                    mix_copy(1)
                if ip:
                    b = parity(ip)
                    act.wait_ge(s["patch_done"], value(ip, 1, 1))
                    if first(ip, 1):
                        act.wait_ge(s["grid_init"], 2)
                    if not first(ip, 2):
                        act.wait_ge(s["tok_done"], value(ip, 1, -1))
                    bias = par("patch_bias")
                    nc.scalar.activation(grid_sb[:, b, :], patch_ps, ACT.Identity, bias=bias)
                    square_ps = patch_ps.rearrange("p (i j) -> p i j", i=GRID)
                    for dst, rows_to, rows_from, cols_to, cols_from, src in (
                            (64, (0, GRID), (0, GRID), (1, GRID), (0, GRID - 1), 64),
                            (96, (0, GRID), (0, GRID), (0, GRID - 1), (1, GRID), 96),
                            (0, (1, GRID), (0, GRID - 1), (0, GRID), (0, GRID), 64),
                            (32, (0, GRID - 1), (1, GRID), (0, GRID), (0, GRID), 96)):
                        ins = nc.scalar.activation(
                            near_sb[dst:dst + 32, b, rows_to[0]:rows_to[1], cols_to[0]:cols_to[1]],
                            square_ps[src:src + 32, rows_from[0]:rows_from[1], cols_from[0]:cols_from[1]],
                            ACT.Identity, bias=bias[src:src + 32])
                    ins.then_inc(s["grid_done"], 1)
                if ia:
                    v_copy(ia, 0)
                if is_:
                    mix_copy(2)
                if il:
                    if not first(il, 2):
                        act.wait_ge(s["nt_done"], value(il, 1, -1))
                        act.wait_ge(norm_moved[parity(il)], 48 * half_number(il))
                    norm_apply(1, il, lambda t: normed[:, parity(il), t, :], "normed_s")

            act.dma_start(x_sb[:, 0, :, :], x[0]).then_inc(x_in[0], 16)
            act.dma_start(const_sb[:, :], consts).then_inc(s["const_in"], 16)
            act.wait_ge(s["const_in"], 16)
            act.wait_ge(s["par_in"], 16)
            act.wait_ge(s["v_init"], 1)
            run_images(act, step)

            def gelu(m, off, again):
                i = 2 * m + off
                for c in range(IC):
                    act.wait_ge(s["hid_done"], IC * i + (c + 1))
                    if again and c == 0:
                        act.wait_ge(s["shared_done"], i - 1)
                    nc.scalar.activation(gelu_sb[:, off, c, :], quad[:, c, 0:TOKENS],
                                         ACT.Gelu).then_inc(s["gelu_done"], 1)
            gelu(0, 0, False)
            gelu(0, 1, False)
            with act.Fori(1, IMAGES // 2) as m:
                gelu(m, 0, True)
                gelu(m, 1, True)

            def row_t_copy(j, b, again):
                act.wait_ge(s["row_t_done"], j + 1)
                if again:
                    act.wait_ge(s["up_done"], 2 * j - 2)
                nc.scalar.activation(row_t[:, b, :], row_t_ps,
                                     ACT.Copy).then_inc(s["row_t_copied"], 1)

            def silu(j, b, again):
                act.wait_ge(s["up_done"], 2 * j + 1)
                if again:
                    act.wait_ge(s["gated_s"], j - 1)
                nc.scalar.activation(silu_c[:, b, :], silu_ps[b], ACT.Silu).then_inc(s["silu_done"], 1)

            def gated_t_copy(j, b, again):
                act.wait_ge(s["gt_done"], j + 1)
                if again:
                    act.wait_ge(s["down_done"], j - 1)
                nc.scalar.activation(gated_t[:, b, :], gated_t_ps, ACT.Copy).then_inc(s["gt_copied"], 1)

            row_t_copy(0, 0, False)
            row_t_copy(1, 1, False)
            silu(0, 0, False)

            def tile_step(j, b, again, rows_ahead, next_silu):
                if rows_ahead:
                    row_t_copy(j + 2, b, True)
                gated_t_copy(j, b, again)
                if next_silu:
                    silu(j + 1, 1 - b, again)
            tile_step(0, 0, False, True, True)
            tile_step(1, 1, False, True, False)
            act.wait_ge(s["gated_s"], 1)
            silu(2, 0, False)
            with act.Fori(1, SLOT_TILES // 2 - 1) as m:
                for b in range(2):
                    tile_step(2 * m + b, b, True, True, True)
            tile_step(SLOT_TILES - 2, 0, True, False, True)
            tile_step(SLOT_TILES - 1, 1, True, False, False)

        @block.tensor
        def _(pe):
            ident = const("identity")

            def step(st):
                ip, ia, iq, is_, il, ig = (st.get(n) for n in "PAQSLG")
                if is_:
                    bs = parity(is_)

                def v_of(t, w):
                    return v_pad[0:w, bs, t, :, :].rearrange("p (r e) c -> p r (e c)", e=2) \
                        .rearrange("p r (f d) -> p r f d", d=HD)[:, :, 0::3, :]

                def qkv(im, t):
                    if t > 0 or not first(im, 1):
                        pe.wait_ge(s["rot_done"], value(im, 2 * TILES, 2 * t))
                        pe.wait_ge(s["v_done"], value(im, TILES, t))
                    nc.tensor.matmul(qkv_ps, xin_t[:, t, :], qkv_w_sb[:, :],
                                     start=True, stop=True).then_inc(s["qkv_done"], 1)

                def scores(t):
                    w = WIDTH[t]
                    for g in range(2):
                        rows_of = slice(64 * g, 64 * g + 64)
                        mm = nc.tensor.matmul(score_ps(t)[:, g, :, :], k_t[rows_of, t, 0:w],
                                              q_four[rows_of, t, :, 0:w], start=True, stop=True)
                    mm.then_inc(s["scores_done"], 1)

                def mix(t):
                    w = WIDTH[t]
                    if t > 0 or not first(is_, 1):
                        pe.wait_ge(s["mix_copied"], value(is_, TILES, t))
                    if t > 0:
                        nc.tensor.matmul(mix_ps[:, 0:w], state[:, t - 1, :], q_t[:, t, 0:w],
                                         start=True, stop=False)
                    pe.wait_ge(s["probs_done"], value(is_, TILES, t + 1))
                    for e in range(2):
                        for r in range(4):
                            mm = nc.tensor.matmul(mix_ps[32 * r:32 * r + 32, 0:w],
                                                  v_pad[0:w, bs, t, 2 * r + e, :], probs[0:w, t % 2, 2 * r + e, 0:w],
                                                  start=(t == 0 and e == 0), stop=(e == 1))
                    mm.then_inc(s["mix_done"], 1)

                def turn_back(im, t):
                    w = WIDTH[t]
                    pe.wait_ge(s["mix_copied"], value(im, TILES, t + 1))
                    if t == 0:
                        if ig:
                            pe.wait_ge(s["nt_copied"], value(ig, 1, 1))
                        elif iq:
                            pe.wait_ge(s["xt_copied"], value(iq, 1, 1))
                    if t > 0 or not first(im, 1):
                        pe.wait_ge(s["mixed_s"], value(im, TILES, t))
                    nc.tensor.transpose(back_ps[0:w, :], mix_t[:, t % 2, 0:w], ident).then_inc(s["back_done"], 1)

                def patches(lo, hi):
                    b = parity(ip)
                    if lo == 0:
                        pe.wait_ge(x_in[b], 16 * half_number(ip) + 16)
                        if not first(ip, 1):
                            pe.wait_ge(s["tok_normed"], value(ip, 1, 0))
                    for k in range(lo, hi):
                        mm = nc.tensor.matmul(patch_ps, patch_w_sb[:, k, :], x_sb[:, b, k, :],
                                              start=(k == 0), stop=(k == KC - 1))
                    if hi == KC:
                        mm.then_inc(s["patch_done"], 1)

                if il:
                    turn_back(il, 2)
                if is_:
                    pe.wait_ge(s["qk_done"], value(is_, TILES, TILES))
                    if not first(is_, 1):
                        pe.wait_ge(s["q_t_s"], value(is_, 1, 0))
                        pe.wait_ge(s["probs_done"], value(is_, TILES, 0))
                    for t in range(TILES):
                        mm = nc.tensor.transpose(qt_ps[:, t * P:(t + 1) * P], qk[:, bs, 0, t, :], ident)
                    mm.then_inc(s["q_turned"], 1)
                if iq:
                    qkv(iq, 1)
                if is_:
                    pe.wait_ge(s["k_done"], value(is_, 1, 1))
                    for t in range(TILES):
                        mm = nc.tensor.transpose(kt_ps[:, t * P:(t + 1) * P], qk[:, bs, 1, t, :], ident)
                    mm.then_inc(s["k_turned"], 1)
                    pe.wait_ge(s["v_done"], value(is_, TILES, TILES))
                    for n in range(2):
                        for t in range(n + 1):
                            mm = nc.tensor.matmul(state_ps[:, n * P:(n + 1) * P],
                                                  qk[0:HALF, bs, 1, t, :], v_of(t, HALF),
                                                  start=(t == 0), stop=(t == n))
                    mm.then_inc(s["state_done"], 1)
                if ig:
                    pe.wait_ge(s["normed_s"], value(ig, 1, 1))
                    pe.wait_ge(s["xt_copied"], value(iq, 1, 1) if iq else IMAGES)
                    pe.wait_ge(s["mixed_s"], value(is_, TILES, 0) if is_ else TILES * IMAGES)
                    if not first(ig, 1):
                        pe.wait_ge(s["nt_copied"], value(ig, 1, 0))
                    for t in range(TILES):
                        mm = nc.tensor.transpose(xt_ps[:, t * P:(t + 1) * P], normed[:, parity(ig), t, :], ident)
                    mm.then_inc(s["nt_done"], 1)
                if iq:
                    qkv(iq, 2)
                if ip:
                    patches(0, 1)
                if is_:
                    pe.wait_ge(s["k_t_s"], value(is_, 1, 1))
                    pe.wait_ge(s["q_four_s"], value(is_, 4, 4))
                    pe.wait_ge(s["state_masked"], value(is_, 1, 1))
                    scores(0)
                if ig:
                    pe.wait_ge(s["nt_copied"], value(ig, 1, 1))
                    if not first(ig, 1):
                        pe.wait_ge(s["logits_done"], value(ig, 1, 0))
                    if not is_:
                        pe.wait_ge(s["mix_copied"], TILES * IMAGES)
                    elif not first(is_, 1):
                        pe.wait_ge(s["mix_copied"], value(is_, TILES, 0))
                    for t in range(TILES):
                        mm = nc.tensor.matmul(gate_ps[:, t * EXPERTS:(t + 1) * EXPERTS],
                                              normed_t[:, t, :], par("gate"), start=True, stop=True)
                    mm.then_inc(s["gate_done"], 1)
                if ip:
                    patches(1, 2)
                if is_:
                    pe.wait_ge(s["q_t_s"], value(is_, 1, 1))
                    scores(1)
                if ip:
                    patches(2, 5)
                if is_:
                    if ig:
                        pe.wait_ge(s["logits_done"], value(ig, 1, 1))
                    mix(0)
                    scores(2)
                if ia:
                    pe.wait_ge(s["xin_done"], value(ia, 1, 1))
                    if ig:
                        pe.wait_ge(s["nt_copied"], value(ig, 1, 1))
                    if il:
                        pe.wait_ge(s["mixed_s"], value(il, TILES, TILES))
                    if not first(ia, 1):
                        pe.wait_ge(s["xt_copied"], value(ia, 1, 0))
                    for t in range(TILES):
                        mm = nc.tensor.transpose(xt_ps[:, t * P:(t + 1) * P], xin[:, parity(ia), t, :], ident)
                    mm.then_inc(s["xt_done"], 1)
                if ip:
                    patches(5, KC)
                if is_:
                    mix(1)
                if ia:
                    pe.wait_ge(s["xt_copied"], value(ia, 1, 1))
                    if first(ia, 1):
                        pe.wait_ge(s["qkvw_in"], 16)
                    qkv(ia, 0)
                if is_:
                    turn_back(is_, 0)
                    mix(2)
                    turn_back(is_, 1)
                if ip:
                    b = parity(ip)
                    if first(ip, 1):
                        pe.wait_ge(s["const_in"], 16)
                        pe.wait_ge(s["par_in"], 16)
                    pe.wait_ge(s["grid_done"], value(ip, 1, 1))
                    for t in range(2):
                        at = START[t]
                        nc.tensor.matmul(tok_ps[0:HALF, t, :], grid_sb[:, b, at:at + HALF],
                                         const("select_same"), start=True, stop=False)
                        mm = nc.tensor.matmul(tok_ps[0:HALF, t, 4 * HD:8 * HD],
                                              near_sb[:, b, :, :].rearrange("p i j -> p (i j)")[:, at:at + HALF],
                                              const("select_neighbours"), start=False, stop=True)
                    mm.then_inc(s["tok_done"], 1)
            pe.wait_ge(s["w_in"], 16)
            run_images(pe, step)

            pe.wait_ge(s["shared_in"], 32)
            for b in range(2):
                pe.wait_ge(norm_moved[b], 48 * (IMAGES // 2))
            pe.wait_ge(s["probs_done"], TILES * IMAGES)
            pe.wait_ge(s["tok_normed"], IMAGES)
            pe.wait_ge(s["nt_copied"], IMAGES)
            pe.wait_ge(s["mixed_s"], TILES * IMAGES)
            pe.wait_ge(s["logits_done"], IMAGES)

            def hidden(i, again):
                for c in range(IC):
                    if again:
                        pe.wait_ge(s["gelu_done"], IC * i - (IC - 1 - c))
                    nc.tensor.matmul(quad[:, c, 0:TOKENS], sw1_sb[:, c * P:(c + 1) * P],
                                     normed_t_all[:, bass.ds(i * TOKENS, TOKENS)],
                                     start=True, stop=True).then_inc(s["hid_done"], 1)

            def shared(i, b, again):
                pe.wait_ge(s["gelu_done"], IC * i + IC)
                if again:
                    pe.wait_ge(s["base_done"], TILES * i - TILES)
                for t in range(TILES):
                    for c in range(IC):
                        mm = nc.tensor.matmul(bank[b][0:WIDTH[t], t * P:(t + 1) * P],
                                              gelu_sb[:, b, c, START[t]:START[t] + WIDTH[t]],
                                              sw2_sb[:, c, :], start=(c == 0), stop=(c == IC - 1))
                mm.then_inc(s["shared_done"], 1)

            hidden(0, False)

            def route():
                pe.wait_ge(s["onehot_s"], 1)
                flat = onehot[:, :, :].rearrange("p t e -> p (t e)")
                nc.tensor.matmul(bank[2][:, 0:ALL_TILES * EXPERTS], const("before"), flat, start=True, stop=True)
                nc.tensor.matmul(bank[3][:, 0:ALL_TILES * EXPERTS], const("ones"), flat,
                                 start=True, stop=True).then_inc(s["rank_done"], 1)
            hidden(1, True)
            shared(0, 0, False)
            route()
            hidden(2, True)
            shared(1, 1, False)
            with pe.Fori(1, IMAGES // 2 - 1) as m:
                hidden(2 * m + 1, True)
                shared(2 * m, 0, True)
                hidden(2 * m + 2, True)
                shared(2 * m + 1, 1, True)
            hidden(IMAGES - 1, True)
            shared(IMAGES - 2, 0, True)
            shared(IMAGES - 1, 1, True)

            pe.wait_ge(s["expert_in"], 48)
            pe.wait_ge(s["expert_of_tile_s"], 1)
            pe.wait_ge(s["base_done"], ALL_TILES)
            pe.wait_ge(s["pos_done"], 1)

            def row_transpose(m, off):
                pe.wait_ge(row_in[off % 4], 16 * (m + off // 4) + 16)
                if type(m) is not int or m + off > 0:
                    pe.wait_ge(s["row_t_copied"], 4 * m + off)
                nc.tensor.transpose(row_t_ps, row_c[:, off % 4, :], ident).then_inc(s["row_t_done"], 1)

            def expert(j):
                return pe.value_load(expert_of_tile[0:1, bass.ds(j, 1)], min_val=0, max_val=EXPERTS - 1)

            def up(j, e, b, again):
                pe.wait_ge(s["row_t_copied"], j + 1)
                if again:
                    pe.wait_ge(s["silu_done"], j - 1)
                nc.tensor.matmul(silu_ps[b], row_t[:, b, :], w1_sb[:, bass.ds(e * INNER, INNER)],
                                 start=True, stop=True).then_inc(s["up_done"], 1)
                if again:
                    pe.wait_ge(s["gated_s"], j - 1)
                nc.tensor.matmul(gate_ps_c[b], row_t[:, b, :], w3_sb[:, bass.ds(e * INNER, INNER)],
                                 start=True, stop=True).then_inc(s["up_done"], 1)

            def gated_transpose(j, b, again):
                pe.wait_ge(s["gated_s"], j + 1)
                if again:
                    pe.wait_ge(s["gt_copied"], j)
                for c in range(IC):
                    mm = nc.tensor.transpose(gated_t_ps[:, c * P:(c + 1) * P],
                                             gated[:, b, c * P:(c + 1) * P], ident)
                mm.then_inc(s["gt_done"], 1)

            def down(j, e, b, again):
                pe.wait_ge(s["gt_copied"], j + 1)
                if again:
                    pe.wait_ge(s["fin_done"], j - 1)
                for c in range(IC):
                    mm = nc.tensor.matmul(down_ps[b], gated_t[:, b, c * P:(c + 1) * P],
                                          w2_sb[:, bass.ds(e * INNER + c * P, P)],
                                          start=(c == 0), stop=(c == IC - 1))
                mm.then_inc(s["down_done"], 1)

            def tile_step(m, off, again, rows_ahead, up_ahead):
                j, b = 4 * m + off, off % 2
                e = expert(j)
                if up_ahead:
                    e_next = expert(j + 1)
                if rows_ahead:
                    row_transpose(m, off + 2)
                gated_transpose(j, b, again or off > 0)
                if up_ahead:
                    up(j + 1, e_next, 1 - b, again or off > 0)
                down(j, e, b, again)

            row_transpose(0, 0)
            row_transpose(0, 1)
            up(0, expert(0), 0, False)
            for off in range(4):
                tile_step(0, off, off > 1, True, True)
            with pe.Fori(1, SLOT_TILES // 4 - 1) as m:
                for off in range(4):
                    tile_step(m, off, True, True, True)
            for off in range(4):
                tile_step(SLOT_TILES // 4 - 1, off, True, off < 2, off < 3)

        @block.vector
        def _(dve):
            def norm_stats(name, k, im, tiles, width, src):
                settle(dve)
                for t in range(tiles):
                    ins = nc.vector.bn_stats(out=stats[0:width, k, t, :], in_=src(t))
                ins.then_inc(s[name + "_stat"], 1)

            def norm_aggregate(name, k, im, tiles, width):
                dve.wait_ge(s[name + "_stat"], value(im, 1, 1))
                settle(dve)
                for t in range(tiles):
                    ins = nc.vector.bn_aggr(out=meanvar[0:width, k, t, :], in_=stats[0:width, k, t, :])
                ins.then_inc(s[name + "_meanvar"], 1)
                dve.wait_ge(s[name + "_meanvar"], value(im, 1, 1))

            def norm_apply(k, tiles, width, src, dst, power, done_sem):
                for t in range(tiles):
                    ins = nc.vector.tensor_scalar(dst(t), src(t), meanvar[0:width, k, t, 0:1],
                                                  power[0:width, t:t + 1], ALU.subtract, ALU.mult)
                ins.then_inc(s[done_sem], 1)

            def residual_rows(which):
                return lambda t: rows[:, bass.ds(number(which) * TILES + t, 1), P:2 * P].rearrange("p o c -> p (o c)")

            def powers(now, cols, step_sem, free=None):
                def link(k, ins):
                    ins.then_inc(s[step_sem], 1)
                    dve.wait_ge(s[step_sem], value(now, NEWTON, k))
                v, y, y2 = var_sb[:, cols], guess[:, cols], square[:, cols]
                bits = y.bitcast(I32)
                link(1, nc.vector.tensor_scalar(bits, v.bitcast(I32), 1, None,
                                                ALU.logical_shift_right))
                yield
                link(2, nc.vector.tensor_scalar(bits, bits, -1.0, float(0x5f3759df), ALU.mult, ALU.add))
                yield
                for n in range(3):
                    link(3 * n + 3, nc.vector.tensor_tensor(y2, y, y, ALU.mult))
                    yield
                    link(3 * n + 4, nc.vector.scalar_tensor_tensor(
                        out=y2, in0=y2, scalar=-0.5, in1=v,
                        op0=ALU.mult, op1=ALU.mult))
                    yield
                    if n == 2 and free:
                        free()
                    link(3 * n + 5, nc.vector.scalar_tensor_tensor(
                        out=rstd[:, cols] if n == 2 else y, in0=y2, scalar=1.5, in1=y,
                        op0=ALU.add, op1=ALU.mult))
                    yield

            def step(st):
                ip, ia, iq, is_, il, ig = (st.get(n) for n in "PAQSLG")
                now = st["step"]
                past = type(now[0]) is int and now[1] > IMAGES
                if iq:
                    bq = parity(iq)

                def rotate(im, t):
                    dve.wait_ge(s["qkv_done"], value(im, TILES, t + 1))
                    if t > 1 or not first(im, 1):
                        dve.wait_ge(s["qk_done"], value(im, TILES, t - 1))
                    both = qkv_ps[:, 0:2 * P].rearrange("p (a c) -> p a c", a=2)
                    pairs = qkv_ps[:, 0:2 * P].rearrange("p (a c two) -> p a c two", a=2, two=2)
                    cos = const("cos")[:, t * P:(t + 1) * P]
                    sin = const("sin")[:, t * P:(t + 1) * P]
                    nc.vector.tensor_tensor(rot_a[:, rot_buf(im, t), :, :], both,
                                            cos.unsqueeze(1).broadcast_to([P, 2, P]),
                                            ALU.mult).then_inc(s["rot_done"], 1)
                    nc.vector.tensor_tensor(
                        rot_b[:, rot_buf(im, t), :, :].rearrange("p a (c two) -> p a c two", two=2),
                        pairs[:, :, :, ::-1],
                        sin.rearrange("p (c two) -> p c two", two=2).unsqueeze(1)
                        .broadcast_to([P, 2, P // 2, 2]),
                        ALU.mult).then_inc(s["rot_done"], 1)

                def mask(t):
                    w = WIDTH[t]
                    dve.wait_ge(s["scores_done"], value(is_, TILES, t + 1))
                    if t > 1 or not first(is_, 1):
                        dve.wait_ge(s["mix_done"], value(is_, TILES, t - 1 if t > 1 else 0))
                    nc.vector.tensor_tensor(
                        probs[0:w, t % 2, :, 0:w].rearrange("p (g e) n -> p g e n", g=2), score_ps(t),
                        const("causal")[0:w, 0:w].unsqueeze(1).unsqueeze(1).broadcast_to([w, 2, 4, w]),
                        ALU.mult).then_inc(s["probs_done"], 1)

                def residual(im, t):
                    w = WIDTH[t]
                    if t == 0:
                        dve.wait_ge(s["mixed_init"], value(im, 1, 1))
                    dve.wait_ge(s["back_done"], value(im, TILES, t + 1))
                    nc.vector.scalar_tensor_tensor(
                        out=mixed[0:w, t, :], in0=back_ps[0:w, :], scalar=const("gamma_pos")[0:w, t:t + 1],
                        in1=mixed[0:w, t, :], op0=ALU.mult, op1=ALU.add).then_inc(s["mixed_s"], 1)

                if il:
                    residual(il, 2)
                if iq:
                    rotate(iq, 1)
                if ia:
                    dve.wait_ge(s["tok_rstd_s"], value(ia, 1, 1))
                    if not first(ia, 1):
                        dve.wait_ge(s["tok_scaled_s"], value(ia, 1, 0))
                    norm_apply(0, 2, HALF, lambda t: tok_ps[0:HALF, t, :], lambda t: tok_norm[0:HALF, t, :],
                               tok_rstd, "tok_normed")
                if il:
                    if first(il, 1):
                        dve.wait_ge(s["xin_init"], 1)
                    dve.wait_ge(s["mixed_s"], value(il, TILES, TILES))
                    mine = rows[:, bass.ds(number(il) * TILES, TILES), P:2 * P]
                    nc.vector.scalar_tensor_tensor(out=mine, in0=mixed[:, :, :], scalar=0.0, in1=mine,
                                                   op0=ALU.max, op1=ALU.add).then_inc(s["h2_done"], 1)
                if is_:
                    dve.wait_ge(s["state_done"], value(is_, 1, 1))
                    if not first(is_, 1):
                        dve.wait_ge(s["mix_done"], value(is_, TILES, 0))
                    nc.vector.tensor_tensor(state[:, :, :], state_ps.rearrange("p (a c) -> p a c", a=2),
                                            const("block_diag").unsqueeze(1).broadcast_to([P, 2, P]),
                                            ALU.mult).then_inc(s["state_masked"], 1)
                if il:
                    dve.wait_ge(s["h2_done"], value(il, 1, 1))
                    norm_stats("ln2", 2, il, TILES, P, residual_rows(il))
                if iq:
                    rotate(iq, 2)
                if ia:
                    dve.wait_ge(s["h_done"], value(ia, 1, 1))
                    if first(ia, 1):
                        dve.wait_ge(s["txt_in"], 16)
                        dve.wait_ge(s["pad_made"], 3)
                    norm_stats("ln1", 1, ia, TILES, P, residual_rows(ia))
                if type(now[0]) is not int or now[1] > 0:
                    dve.wait_ge(s["shift_s"], value(now, 1, 0))
                if il:
                    norm_aggregate("ln2", 2, il, TILES, P)
                if ia:
                    norm_aggregate("ln1", 1, ia, TILES, P)
                if il:
                    dve.wait_ge(s["ln2_meanvar"], value(il, 1, 1))
                if ia:
                    dve.wait_ge(s["ln1_meanvar"], value(ia, 1, 1))
                if type(now[0]) is not int or now[1] > 0:
                    dve.wait_ge(s["ln_rstd_s"], value(now, 1, 0))
                nc.vector.tensor_scalar(var_sb[:, 0:2 * TILES].rearrange("p (k t) -> p k t", k=2),
                                        meanvar[:, 1:3, :, 1], EPS, None, ALU.add).then_inc(s["norm_vars"], 1)
                dve.wait_ge(s["norm_vars"], value(now, 1, 1))
                if is_:
                    mask(0)
                if ig:
                    dve.wait_ge(s["gate_done"], value(ig, 1, 1))
                    nc.vector.tensor_copy(logits[:, bass.ds(number(ig) * TILES, TILES), :],
                                          gate_ps.rearrange("p (t e) -> p t e", e=EXPERTS)
                                          ).then_inc(s["logits_done"], 1)
                if iq:
                    kk = qk[:, bq, 1, :, :].rearrange("p t (g d) -> p (t g) d", d=HD)
                    dve.wait_ge(s["qk_done"], value(iq, TILES, TILES))
                    nc.vector.tensor_reduce(gn_sum[:, :], kk, AX_X, ALU.add).then_inc(s["gn_sum_s"], 1)
                    dve.wait_ge(s["gn_sum_s"], value(iq, 1, 1))
                    nc.vector.tensor_scalar(gn_mean[:, :], gn_sum[:, :], 1.0 / HD, None,
                                            ALU.mult).then_inc(s["gn_mean_s"], 1)
                dve.wait_ge(s["ln_rstd_s"], value(now, 1, 1))
                if ia and not first(ia, 1):
                    dve.wait_ge(s["xin_done"], value(ia, 1, 0))
                elif past:
                    dve.wait_ge(s["xin_done"], IMAGES)
                if il and not first(il, 1):
                    dve.wait_ge(s["normed_s"], value(il, 1, 0))
                elif past and not il:
                    dve.wait_ge(s["normed_s"], IMAGES)
                nc.vector.scalar_tensor_tensor(out=shift[:, :, :], in0=meanvar[:, 1:3, :, 0], scalar=-1.0,
                                               in1=rstd[:, 0:2 * TILES].rearrange("p (k t) -> p k t", k=2),
                                               op0=ALU.mult, op1=ALU.mult).then_inc(s["shift_s"], 1)
                if is_:
                    mask(1)
                if iq:
                    dve.wait_ge(s["gn_sq_s"], value(iq, 1, 1))
                    nc.vector.tensor_reduce(gn_var[:, :], gn_sq[:, :].rearrange("p (g d) -> p g d", d=HD),
                                            AX_X, ALU.add).then_inc(s["gn_var_s"], 1)
                    dve.wait_ge(s["gn_var_s"], value(iq, 1, 1))
                nc.vector.tensor_scalar(var_sb[:, 2 * TILES:NORMS], gn_var[:, :], 1.0 / HD, EPS,
                                        ALU.mult, ALU.add).then_inc(s["k_vars"], 1)
                dve.wait_ge(s["k_vars"], value(now, 1, 1))

                def k_free():
                    if iq and not first(iq, 1):
                        dve.wait_ge(s["k_norm_s"], value(iq, 1, 0))
                    elif past:
                        dve.wait_ge(s["k_norm_s"], IMAGES)
                newton = powers(now, slice(2 * TILES, NORMS), "newton_k", k_free)
                for k in range(NEWTON):
                    next(newton)
                    if k == 1 and is_:
                        mask(2)
                    if k == 5 and is_:
                        residual(is_, 0)
                if ia:
                    rotate(ia, 0)
                if is_:
                    residual(is_, 1)
                if ip:
                    dve.wait_ge(s["tok_done"], value(ip, 1, 1))
                    norm_stats("tok", 0, ip, 2, HALF, lambda t: tok_ps[0:HALF, t, :])
                    norm_aggregate("tok", 0, ip, 2, HALF)
                    dve.wait_ge(s["tok_meanvar"], value(ip, 1, 1))
                    if not first(ip, 1):
                        dve.wait_ge(s["tok_rstd_s"], value(ip, 1, 0))
                    nc.vector.tensor_scalar(tok_var[0:HALF, :], meanvar[0:HALF, 0, 0:2, 1],
                                            EPS, None, ALU.add).then_inc(s["tok_vareps"], 1)

            nc.vector.memset(near_sb[:, :, :, :], 0.0).then_inc(s["grid_init"], 1)
            dve.wait_ge(s["par_in"], 16)
            dve.wait_ge(s["const_in"], 16)
            dve.wait_ge(s["grid_init"], 1)
            flat = near_sb[:, :, :, :].rearrange("p a i j -> p (a i j)")
            nc.vector.tensor_scalar(flat, flat, par("near_bias"), None, ALU.add).then_inc(s["grid_init"], 1)
            nc.vector.memset(meanvar[:, :, :, :], 1.0).then_inc(s["grid_init"], 1)
            nc.vector.memset(gn_var[:, :], 1.0).then_inc(s["grid_init"], 1)
            dve.wait_ge(s["grid_init"], 4)
            run_images(dve, step)

            done = [0]

            def link(ins):
                done[0] += 1
                ins.then_inc(s["route_step"], 1)
                dve.wait_ge(s["route_step"], done[0])

            def over_experts(ap):
                return ap.unsqueeze(2).broadcast_to([ap.shape[0], ap.shape[1], EXPERTS])

            dve.wait_ge(s["logits_done"], IMAGES)
            link(nc.vector.tensor_reduce(rt_m[:, :], logits[:, :, :], AX_X, ALU.max))
            link(nc.vector.tensor_tensor(rt_eq[:, :, :], logits[:, :, :], over_experts(rt_m[:, :]), ALU.is_equal))
            link(nc.vector.tensor_tensor(rt_cand[:, :, :], rt_eq[:, :, :],
                                         const("descending").unsqueeze(1).broadcast_to([P, ALL_TILES, EXPERTS]),
                                         ALU.mult))
            link(nc.vector.tensor_reduce(rt_best[:, :], rt_cand[:, :, :], AX_X, ALU.max))
            link(nc.vector.tensor_tensor(rt_hit[:, :, :], rt_cand[:, :, :], over_experts(rt_best[:, :]), ALU.is_equal))
            nc.vector.tensor_tensor(
                onehot[:, :, :].rearrange("p (b t) e -> p b t e", t=TILES),
                rt_hit[:, :, :].rearrange("p (b t) e -> p b t e", t=TILES),
                over_experts(const("valid")).unsqueeze(1).broadcast_to([P, IMAGES, TILES, EXPERTS]),
                ALU.mult).then_inc(s["onehot_s"], 1)
            link(nc.vector.memset(rt_zero[:, :], 0.0))
            dve.wait_ge(s["rank_done"], 1)
            link(nc.vector.tensor_copy(rt_tot[:, :, :],
                                       bank[3][:, 0:ALL_TILES * EXPERTS].rearrange("p (t e) -> p e t", e=EXPERTS)))
            link(nc.vector.tensor_tensor_scan(rt_cum[:, :, :].rearrange("p e t -> p (e t)"),
                                              rt_tot[:, :, :].rearrange("p e t -> p (e t)"), rt_zero[:, :],
                                              0.0, ALU.add, ALU.add))
            link(nc.vector.tensor_tensor(rt_exc[:, :, :], rt_cum[:, :, :], rt_tot[:, :, :], ALU.subtract))
            link(nc.vector.tensor_reduce(rt_n[:, :], rt_tot[:, :, :], AX_X, ALU.add))
            link(nc.vector.tensor_scalar(rt_int[:, :], rt_n[:, :], float(P - 1), None, ALU.add))
            link(nc.vector.tensor_scalar(rt_mod[:, :], rt_int[:, :], -P, None, ALU.bitwise_and))
            link(nc.vector.tensor_copy(rt_pad[:, :], rt_mod[:, :]))
            link(nc.vector.tensor_tensor_scan(rt_end[:, :], rt_pad[:, :], rt_zero[:, 0:EXPERTS],
                                              0.0, ALU.add, ALU.add))
            link(nc.vector.tensor_tensor(rt_off[:, :], rt_end[:, :], rt_pad[:, :], ALU.subtract))
            link(nc.vector.tensor_tensor(rt_off2[:, :], rt_off[:, :], rt_exc[:, :, 0], ALU.subtract))
            link(nc.vector.tensor_tensor(rt_base[:, :, :], rt_exc[:, :, :],
                                         rt_off2[:, :].unsqueeze(2).broadcast_to([P, EXPERTS, ALL_TILES]), ALU.add))
            link(nc.vector.tensor_tensor(rt_pos[:, :, :],
                                         bank[2][:, 0:ALL_TILES * EXPERTS].rearrange("p (t e) -> p t e", e=EXPERTS),
                                         rt_base[:, :, :].rearrange("p e t -> p t e"), ALU.add))
            link(nc.vector.tensor_tensor(rt_eq[:, :, :], rt_pos[:, :, :], onehot[:, :, :], ALU.mult))
            link(nc.vector.tensor_reduce(rt_posf[:, :], rt_eq[:, :, :], AX_X, ALU.add))
            nc.vector.tensor_copy(slot_of[:, :], rt_posf[:, :]).then_inc(s["pos_done"], 1)
            link(nc.vector.tensor_tensor(rt_ge[:, :, :], over_experts(const("tile_start")),
                                         rt_end[:, :].unsqueeze(1).broadcast_to([P, SLOT_TILES, EXPERTS]), ALU.is_ge))
            link(nc.vector.tensor_reduce(rt_te[:, :], rt_ge[:, :, :], AX_X, ALU.add))
            nc.vector.tensor_scalar(expert_of_tile[:, :], rt_te[:, :], float(EXPERTS - 1), None,
                                    ALU.min).then_inc(s["expert_of_tile_s"], 1)

            with dve.Fori(0, IMAGES // 2) as m:
                for b in range(2):
                    dve.wait_ge(s["shared_done"], 2 * m + (b + 1))
                    for t in range(TILES):
                        w = WIDTH[t]
                        mine = rows[0:w, bass.ds((2 * m + b) * TILES + t, 1), P:2 * P].rearrange("p o c -> p (o c)")
                        nc.vector.tensor_tensor(mine, bank[b][0:w, t * P:(t + 1) * P], mine,
                                                ALU.add).then_inc(s["base_done"], 1)

            def gate(j, b, again):
                dve.wait_ge(s["silu_done"], j + 1)
                dve.wait_ge(s["up_done"], 2 * j + 2)
                if again:
                    dve.wait_ge(s["gt_done"], j - 1)
                nc.vector.tensor_tensor(gated[:, b, :], silu_c[:, b, :], gate_ps_c[b], ALU.mult).then_inc(s["gated_s"], 1)

            def finish(m, off, again):
                dve.wait_ge(s["down_done"], 4 * m + (off + 1))
                if again:
                    dve.wait_ge(out_sent[off], 16 * m)
                j = 4 * m + off
                nc.vector.tensor_copy(fin_c[:, off, P:P + 1].bitcast(I32),
                                      rows[:, bass.ds(j, 1), ROW_ID:ROW_ID + 1]
                                      .rearrange("p o c -> p (o c)").bitcast(I32))
                nc.vector.tensor_tensor(fin_c[:, off, 0:P], down_ps[off % 2],
                                        rows[:, bass.ds(j, 1), P:2 * P].rearrange("p o c -> p (o c)"),
                                        ALU.add).then_inc(s["fin_done"], 1)

            gate(0, 0, False)
            for off in range(4):
                gate(off + 1, (off + 1) % 2, off > 0)
                if off == 0:
                    dve.wait_ge(rest_in[0], 16)
                finish(0, off, False)
            dve.wait_ge(rest_in[1], 16)
            with dve.Fori(1, SLOT_TILES // 4 - 1) as m:
                for off in range(4):
                    gate(4 * m + (off + 1), (off + 1) % 2, True)
                    finish(m, off, True)
            for off in range(4):
                if off < 3:
                    gate(SLOT_TILES - 4 + off + 1, (off + 1) % 2, True)
                finish(SLOT_TILES // 4 - 1, off, True)


def constants():
    f = np.float32
    c = np.zeros((P, CONST_COLS), f)

    def put(name, a):
        lo, hi = CONST_AT[name]
        c[:, lo:hi] = a
    i = np.arange(P)
    put("identity", np.eye(P))
    put("causal", i[None, :] >= i[:, None])
    put("block_diag", i[:, None] // HD == i[None, :] // HD)
    put("before", i[:, None] < i[None, :])
    put("ones", 1.0)
    same = np.zeros((P, P), f)
    same[:64, :64] = np.eye(64)
    eye = np.eye(HD)
    A, AY, B, BY = 64, 80, 96, 112
    for src, dst in ((A, 64), (B, 80), (AY, 96), (BY, 112)):
        same[src:src + HD, dst:dst + HD] = eye
    put("select_same", same)
    near = np.zeros((P, 4 * HD), f)
    for n, src in enumerate((B, A, BY - 64, AY - 64)):
        near[src:src + HD, n * HD:(n + 1) * HD] = eye
    put("select_neighbours", near)
    half = P // 2
    scale_vec = (np.arange(0, P, 2, dtype=f) + f(0.4 * P)) / f(1.4 * P)
    s = np.arange(TOKENS, dtype=f)
    scale = scale_vec[None, :] ** (s / f(512.0))[:, None]
    inv_freq = f(1.0) / f(10000.0) ** (np.arange(half, dtype=f) / f(half))
    angle = s[:, None] * inv_freq[None, :]
    sin = np.repeat(np.sin(angle) * scale, 2, axis=-1)
    cos = np.repeat(np.cos(angle) * scale, 2, axis=-1)
    sin[:, 0::2] *= -1
    for t in range(TILES):
        w, a = WIDTH[t], START[t]
        for name, table in (("cos", cos), ("sin", sin)):
            lo = CONST_AT[name][0] + t * P
            c[:w, lo:lo + P] = table[a:a + w]
        pos = np.arange(a, a + w, dtype=np.float64)
        c[:w, CONST_AT["gamma_neg"][0] + t] = GAMMA ** -pos
        c[:w, CONST_AT["gamma_pos"][0] + t] = GAMMA ** pos
        c[:w, CONST_AT["valid"][0] + t] = 1.0
    put("head_of_four", i[:, None] % 64 // HD == np.arange(4)[None, :])
    put("descending", EXPERTS - np.arange(EXPERTS)[None, :])
    put("minus_half", -0.5)
    put("tile_start", P * np.arange(SLOT_TILES)[None, :])
    return c


def lay_out(inp):
    x = inp["x"].reshape(IMAGES, 3, GRID, 16, GRID, 16).transpose(0, 1, 3, 5, 2, 4)
    x = x.reshape(IMAGES, KC, P, PATCHES).transpose(0, 2, 1, 3)
    zero = np.zeros((HD, 3, 8, 16), np.float32)
    sx = inp["L0_tok_W_sx"].reshape(HD, 3, 16, 16)
    sy = inp["L0_tok_W_sy"].reshape(HD, 3, 16, 16)
    zx = zero.transpose(0, 1, 3, 2)
    a = np.concatenate([zx, sx[..., :8]], axis=3)
    b = np.concatenate([sx[..., 8:], zx], axis=3)
    ay = np.concatenate([zero, sy[:, :, :8]], axis=2)
    by = np.concatenate([sy[:, :, 8:], zero], axis=2)
    w = np.concatenate([inp["L0_tok_W_main"]] + [m.reshape(HD, 768) for m in (a, ay, b, by)])
    params = np.zeros((P, PAR_COLS), np.float32)
    params[:, 0] = np.concatenate([inp["L0_tok_b_main"], inp["L0_tok_b_sx"], inp["L0_tok_b_sy"],
                                   np.zeros(2 * HD, np.float32)])
    params[:, 1] = np.concatenate([params[64:, 0], params[64:, 0]])
    for name, key in (("ln_g", "L0_tok_ln_g"), ("ln_b", "L0_tok_ln_b"),
                      ("gn_w", "L0_attn_gn_weight"), ("gn_b", "L0_attn_gn_bias")):
        lo, hi = PAR_AT[name]
        params[:, lo:hi] = inp[key][None, :]
    lo, hi = PAR_AT["gate"]
    params[:, lo:hi] = inp["L0_ffn_gate_w"].T
    return {
        "x": x,
        "txt": inp["txt"],
        "patch_w": w.T.reshape(KC, P, P).transpose(1, 0, 2),
        "params": params,
        "w_qkv": np.concatenate([inp["L0_attn_Wq"], inp["L0_attn_Wk"], inp["L0_attn_Wv"]], axis=1),
        "w1": inp["L0_ffn_w1"].transpose(2, 0, 1).reshape(P, EXPERTS * INNER),
        "w3": inp["L0_ffn_w3"].transpose(2, 0, 1).reshape(P, EXPERTS * INNER),
        "w2": inp["L0_ffn_w2"].reshape(EXPERTS, P, IC, P).transpose(3, 0, 2, 1).reshape(P, EXPERTS * INNER),
        "sw1": inp["L0_ffn_sw1"].T,
        "sw2": inp["L0_ffn_sw2"].reshape(P, IC, P).transpose(2, 1, 0),
        "consts": constants(),
    }


def kernel(**inputs):
    import concourse.bacc as bacc
    from concourse.bass_utils import run_bass_kernel_spmd

    nc = bacc.Bacc("TRN2", target_bir_lowering=False, num_devices=1)
    arrays, args = {}, []
    for name, a in lay_out({k: np.asarray(v) for k, v in inputs.items()}).items():
        a = np.ascontiguousarray(a)
        arrays[f"in_{name}"] = a
        args.append(nc.dram_tensor(f"in_{name}", a.shape, mybir.dt.from_np(a.dtype), kind="ExternalInput").ap())
    args.append(nc.dram_tensor("out", (IMAGES, TOKENS, P), F32, kind="ExternalOutput").ap())
    build(nc, *args)
    r = run_bass_kernel_spmd(nc, [arrays], core_ids=[0])
    return r.results[0]["out"]
```
